# Optimizing a Trainium2 kernel written in Bass

```python
import numpy as np
import jax
import jax.numpy as jnp

def _softmax(x, axis=-1):
    return jax.nn.softmax(x, axis=axis)

def _gelu(x):
    return jax.nn.gelu(x, approximate=True)

def _silu(x):
    return jax.nn.silu(x)

def _sigmoid(x):
    return jax.nn.sigmoid(x)

def _layernorm(x, axis=-1, eps=1e-05):
    m = jnp.mean(x, axis=axis, keepdims=True)
    v = jnp.var(x, axis=axis, keepdims=True)
    return (x - m) / jnp.sqrt(v + eps)

def _scatter_add(tgt, idx, src, axis=0):
    return tgt.at[idx].add(src)

def _segment_sum(src, seg, n):
    return jax.ops.segment_sum(src, seg, n)
kernel_name = 'mk_prb_d1_jaxref_r4_ee1492'

def setup_inputs(seed: int=0):
    np.random.seed(seed)
    _w = jnp.asarray

    def _L0_attn_setup():
        import jax, jax.numpy as jnp
        import numpy as np
        D_MODEL = 256
        NUM_HEADS = 16
        HEAD_DIM = D_MODEL // NUM_HEADS
        LN_EPS = 1e-05

        def _layernorm(x, gamma, beta):
            mu = jnp.mean(x, axis=-1, keepdims=True)
            var = jnp.mean(jnp.square(x - mu), axis=-1, keepdims=True)
            return (x - mu) * jax.lax.rsqrt(var + LN_EPS) * gamma + beta
        key = jax.random.key(seed)
        ks = jax.random.split(key, 7)
        B, S, D = (2, 512, D_MODEL)
        x = jax.random.normal(ks[0], (B, S, D), dtype=jnp.float32)
        lim1 = 1.0 / np.sqrt(D)
        W1 = jax.random.uniform(ks[1], (D, 4 * D), minval=-lim1, maxval=lim1, dtype=jnp.float32)
        b1 = jax.random.uniform(ks[2], (4 * D,), minval=-lim1, maxval=lim1, dtype=jnp.float32)
        W2 = jax.random.uniform(ks[3], (D, D), minval=-lim1, maxval=lim1, dtype=jnp.float32)
        b2 = jax.random.uniform(ks[4], (D,), minval=-lim1, maxval=lim1, dtype=jnp.float32)
        gamma = jnp.ones((D,), dtype=jnp.float32)
        beta = jnp.zeros((D,), dtype=jnp.float32)
        return {'x': x, 'W1': W1, 'b1': b1, 'W2': W2, 'b2': b2, 'gamma': gamma, 'beta': beta}
    _L0_attn_in = _L0_attn_setup()

    def _L0_ffn_setup():
        import jax, jax.numpy as jnp
        import numpy as np
        LN_EPS = 1e-05

        def layer_norm(x, g, b):
            mu = jnp.mean(x, axis=-1, keepdims=True)
            var = jnp.mean(jnp.square(x - mu), axis=-1, keepdims=True)
            return (x - mu) * jax.lax.rsqrt(var + LN_EPS) * g + b

        def ternary_quant(w):
            scale = 1.0 / jnp.clip(jnp.mean(jnp.abs(w)), 1e-05)
            wq = jnp.clip(jnp.round(w * scale), -1.0, 1.0) / scale
            return w + jax.lax.stop_gradient(wq - w)
        key = jax.random.key(seed)
        ks = jax.random.split(key, 3)
        dim, hidden = (256, 1024)
        B, S = (8, 256)
        x = jax.random.normal(ks[0], (B, S, dim), dtype=jnp.float32)
        w1 = jax.random.normal(ks[1], (hidden, dim), dtype=jnp.float32) * 0.02
        w2 = jax.random.normal(ks[2], (dim, hidden), dtype=jnp.float32) * 0.02
        return {'x': x, 'ln1_g': jnp.ones((dim,), jnp.float32), 'ln1_b': jnp.zeros((dim,), jnp.float32), 'w1': w1, 'b1': jnp.zeros((hidden,), jnp.float32), 'ln2_g': jnp.ones((hidden,), jnp.float32), 'ln2_b': jnp.zeros((hidden,), jnp.float32), 'w2': w2, 'b2': jnp.zeros((dim,), jnp.float32)}
    _L0_ffn_in = _L0_ffn_setup()
    _d = {'L0_attn_x': _L0_attn_in['x'], 'L0_attn_W1': _L0_attn_in['W1'], 'L0_attn_b1': _L0_attn_in['b1'], 'L0_attn_W2': _L0_attn_in['W2'], 'L0_attn_b2': _L0_attn_in['b2'], 'L0_attn_gamma': _L0_attn_in['gamma'], 'L0_attn_beta': _L0_attn_in['beta'], 'L0_ffn_ln1_g': _L0_ffn_in['ln1_g'], 'L0_ffn_ln1_b': _L0_ffn_in['ln1_b'], 'L0_ffn_w1': _L0_ffn_in['w1'], 'L0_ffn_b1': _L0_ffn_in['b1'], 'L0_ffn_ln2_g': _L0_ffn_in['ln2_g'], 'L0_ffn_ln2_b': _L0_ffn_in['ln2_b'], 'L0_ffn_w2': _L0_ffn_in['w2'], 'L0_ffn_b2': _L0_ffn_in['b2']}
    _x0 = _d['L0_attn_x']
    _d['L0_attn_x'] = jax.random.normal(jax.random.fold_in(jax.random.key(seed), 1), (8, 1024, 256), dtype=_x0.dtype)
    del _x0
    return _d

def reference(L0_attn_x, L0_attn_W1, L0_attn_b1, L0_attn_W2, L0_attn_b2, L0_attn_gamma, L0_attn_beta, L0_ffn_ln1_g, L0_ffn_ln1_b, L0_ffn_w1, L0_ffn_b1, L0_ffn_ln2_g, L0_ffn_ln2_b, L0_ffn_w2, L0_ffn_b2):

    def _L0_attn_ref(x, W1, b1, W2, b2, gamma, beta):
        import jax, jax.numpy as jnp
        import numpy as np
        D_MODEL = 256
        NUM_HEADS = 16
        HEAD_DIM = D_MODEL // NUM_HEADS
        LN_EPS = 1e-05

        def _layernorm(x, gamma, beta):
            mu = jnp.mean(x, axis=-1, keepdims=True)
            var = jnp.mean(jnp.square(x - mu), axis=-1, keepdims=True)
            return (x - mu) * jax.lax.rsqrt(var + LN_EPS) * gamma + beta
        B, S, D = x.shape
        H, Dh = (NUM_HEADS, HEAD_DIM)
        x_proj = jax.nn.silu(x @ W1 + b1)
        u, v, q, k = jnp.split(x_proj, 4, axis=-1)
        qh = q.reshape(B, S, H, Dh)
        kh = k.reshape(B, S, H, Dh)
        vh = v.reshape(B, S, H, Dh)
        scores = jnp.einsum('bqhd,bkhd->bhqk', qh, kh)
        attn = jax.nn.silu(scores) / S
        av = jnp.einsum('bhqk,bkhd->bqhd', attn, vh).reshape(B, S, D)
        y = _layernorm(av * u, gamma, beta) @ W2 + b2
        return y

    def _L0_ffn_ref(x, ln1_g, ln1_b, w1, b1, ln2_g, ln2_b, w2, b2):
        import jax, jax.numpy as jnp
        import numpy as np
        LN_EPS = 1e-05

        def layer_norm(x, g, b):
            mu = jnp.mean(x, axis=-1, keepdims=True)
            var = jnp.mean(jnp.square(x - mu), axis=-1, keepdims=True)
            return (x - mu) * jax.lax.rsqrt(var + LN_EPS) * g + b

        def ternary_quant(w):
            scale = 1.0 / jnp.clip(jnp.mean(jnp.abs(w)), 1e-05)
            wq = jnp.clip(jnp.round(w * scale), -1.0, 1.0) / scale
            return w + jax.lax.stop_gradient(wq - w)
        h = layer_norm(x, ln1_g, ln1_b)
        h = jnp.einsum('bsd,hd->bsh', h, ternary_quant(w1)) + b1
        h = jax.nn.gelu(h, approximate=False)
        h = layer_norm(h, ln2_g, ln2_b)
        out = jnp.einsum('bsh,dh->bsd', h, ternary_quant(w2)) + b2
        return out
    x = L0_attn_x
    xn = _layernorm(x, axis=-1)
    x = x + _L0_attn_ref(xn, L0_attn_W1, L0_attn_b1, L0_attn_W2, L0_attn_b2, L0_attn_gamma, L0_attn_beta) + _L0_ffn_ref(xn, L0_ffn_ln1_g, L0_ffn_ln1_b, L0_ffn_w1, L0_ffn_b1, L0_ffn_ln2_g, L0_ffn_ln2_b, L0_ffn_w2, L0_ffn_b2)
    return x

_drawn_inputs = setup_inputs


def setup_inputs(seed=0):
    import zlib

    import numpy as np

    out = dict(_drawn_inputs(seed))
    spreads = {'L0_attn_gamma': (1.0, 0.2),
     'L0_attn_beta': (0.0, 0.1),
     'L0_ffn_ln1_g': (1.0, 0.2),
     'L0_ffn_ln1_b': (0.0, 0.1),
     'L0_ffn_b1': (0.0, 0.1),
     'L0_ffn_ln2_g': (1.0, 0.2),
     'L0_ffn_ln2_b': (0.0, 0.1),
     'L0_ffn_b2': (0.0, 0.1)}
    factors = {}
    for name, (base, spread) in spreads.items():
        noise = np.random.default_rng([zlib.crc32(name.encode()), seed]).standard_normal(out[name].shape)
        drawn = base * np.exp(spread * noise) if base else spread * noise
        out[name] = jnp.asarray(drawn.astype(out[name].dtype))
    for name, factor in factors.items():
        out[name] = (out[name] * factor).astype(out[name].dtype)
    return out
```

```python
import numpy as np

import concourse.bass as bass
from concourse import mybir
from contextlib import ExitStack

F32 = mybir.dt.float32
F32R = mybir.dt.float32r
BF16 = mybir.dt.bfloat16
ALU = mybir.AluOpType
ACT = mybir.ActivationFunctionType

P = 128
NB, SEQ, D = 8, 1024, 256
HEADS, DH = 16, 16
HID = 1024
EPS = 1e-5
DC = D // P
HC = HID // P
T = SEQ // P
HPC = P // DH
HALF = 512
NH = SEQ // HALF
PAIR = 2 * P
NP = T // 2
PARTS = 3
QROWS = PARTS * DH
KROWS = (PARTS + 2) * DH
GROUPS = DC * NH * 2 * T
PHASE = GROUPS // DC
RUN = 2 * T
ROUND = 1.5 * 2.0 ** 23

SLOTS = {g: [] for g in range(GROUPS)}


def put(slot, kind, *args):
    SLOTS[slot].append((kind, *args))


for _i in range(NP):
    put(2 + _i // 2, "zt", _i), put(4 + _i, "a", _i)
put(2, "vs", 1)
for _i in range(NH):
    for _n, _k in enumerate(("k", "q")):
        put(8 + 2 * _i + _n, _k, 1, _i), put(8 + 2 * _i + _n, "u", _i, _n)
put(7, "hn", 0), put(9, "h", 0), put(10, "hn", 1), put(10, "px")
for _n in range(4):
    put(11 + (_n + 1) // 2, "f1", _n // 2, _n % 2)
put(13, "h", 1)
GELU = [14, 23, 32, 41]
for _i, s in enumerate(GELU):
    put(s, "gelu", _i)
    if _i < NP - 1:
        for _n in range(4):
            put(s + _n // 2, "f1", 2 * _i + 2 + _n // 2, _n % 2)
    put(s + 1, "ln2", _i), put(s + 3, "nrm2", _i)
    if _i < NP - 2:
        put(s + 6, "hn", _i + 2), put(s + 8, "h", _i + 2)
    if _i != NP - 2:
        put(s + 4, "g", 2 * _i, 0), put(s + 5, "g", 2 * _i, 1), put(s + 6, "f2", 2 * _i)
        put(s + 6, "g", 2 * _i + 1, 0), put(s + 7, "g", 2 * _i + 1, 1), put(s + (9 if _i < NP - 1 else 8), "f2", 2 * _i + 1)
    else:
        put(s + 5, "g", 2 * _i, 0), put(s + 6, "g", 2 * _i, 1), put(s + 9, "f2", 2 * _i)
        put(s + 9, "g", 2 * _i + 1, 0), put(s + 9, "g", 2 * _i + 1, 1), put(s + 10, "f2", 2 * _i + 1)
put(40, "ln1"), put(49, "xn", 0)
for _i in range(NP):
    if _i < NP - 1:
        put(50 + _i, "xn", _i + 1)
    put(50 + _i, "xt", _i)
put(52, "k", 0, 0), put(53, "q", 0, 0), put(54, "k", 0, 1), put(55, "q", 0, 1)
for _i, s in enumerate((57, 59, 61, 62)):
    put(s, "v", _i)
put(63, "vs", 0)

POST = ("zt", "a")



def is_next(s):
    return s[0] in ("ln1", "xn", "xt", "v") or s[0] in ("k", "q") and s[1] == 0


FILLERS = ("zt", "a", "u", "h", "f1", "g", "f2", "xt", "k", "q", "v")
ORDER = [s for g in range(GROUPS) for s in SLOTS[g]]
PIECES = [s for s in ORDER if s[0] in FILLERS]
POS = {s: n for n, s in enumerate(PIECES)}
NPOST = sum(s[0] in POST for s in PIECES)
NNEXT = sum(is_next(s) for s in PIECES)
NPIECES = len(PIECES)
assert NPIECES % 2 == 0 and NPOST % 2 == 0 and NNEXT % 2 == 0
assert all(POS[s] < NPOST for s in PIECES if s[0] in POST)
assert all(POS[s] >= NPIECES - NNEXT for s in PIECES if is_next(s))


def bank_of(step):
    return POS[step] % 2


def turn_of(body, step):
    n = POS[step] // 2 + 1
    if isinstance(body, int) and body < 0:
        return n - (NPIECES - NNEXT) // 2
    base = body * (NPIECES // 2) + (NNEXT - NPOST) // 2
    if isinstance(body, int) and body == NB:
        base = base - NNEXT // 2
    return base + n


def hybrid_block_kernel(nc, x, W1, b1, b1c, W2, b2, gamc, betc, l1gc, l1bc, w1T, fb1, l2gc, l2bc, w2T, fb2, out):
    xv = x.rearrange("b (p t) d -> b p t d", p=P)
    ov = out.rearrange("b (p t) d -> b p t d", p=P)
    kd = [nc.dram_tensor(f"k_scratch{c}", [HPC, KROWS, SEQ], BF16, kind="Internal").ap() for c in range(DC)]
    qd = [nc.dram_tensor(f"q_scratch{c}", [HPC, QROWS, SEQ], BF16, kind="Internal").ap() for c in range(DC)]

    ctx = ExitStack()
    with ctx:
        top = [nc.sbuf_base + (-nc.sbuf_base) % 64]

        def at(name, shape, dt, offset):
            return nc.alloc_sbuf_tensor_at(name, shape, dt, offset=offset)

        def sb(name, shape, dt):
            offset = top[0]
            size = int(np.prod(shape[1:])) * (2 if dt == BF16 else 4)
            top[0] = offset + size + (-size) % 32
            return at(name, shape, dt, offset)

        QS = sb("QS", [P, HEADS, SEQ], BF16)
        KS = sb("KS", [P, HEADS, SEQ], BF16)
        V = sb("V", [P, T, HEADS // 2, 3 * DH], F32)
        uz = sb("uz", [P, DC, SEQ], F32)
        attn_at = top[0]
        attn = sb("attn", [P, 2, 4, HALF], F32)
        W1h = sb("W1h", [P, DC, 4 * D], F32R)
        W1l = sb("W1l", [P, DC, 4 * D], F32R)
        Wq1 = sb("Wq1", [P, DC, HID], F32R)
        Wq2 = sb("Wq2", [P, HC, D], F32R)
        W2c = sb("W2c", [P, DC, D], F32)
        vraw = sb("vraw", [P, T, D], F32)
        xh_at = top[0]
        xh = sb("xh", [P, DC, SEQ], F32R)
        xl = sb("xl", [P, DC, SEQ], F32R)
        hid = at("hid", [P, 4, HID], F32, xh_at)
        hTh = sb("hTh", [P, DC, PAIR], F32R)
        hTl = sb("hTl", [P, DC, PAIR], F32R)
        hgh = sb("hgh", [P, 2, HALF], F32R)
        hgl = sb("hgl", [P, 2, HALF], F32R)
        part_at = top[0]
        part = sb("part", [P, T, D], F32)
        xin = sb("xin", [P, T, D], F32)
        fb1b = sb("fb1b", [P, HID], F32)
        kst = sb("kst", [P, PARTS, HALF], BF16)
        qst = sb("qst", [P, PARTS, HALF], BF16)
        qkf = sb("qkf", [P, HALF], F32)
        normed = sb("normed", [P, 2, D], F32)
        tmp = sb("tmp", [P, HALF], F32)
        bvb = sb("bvb", [P, D], F32)
        cst = sb("cst", [P, D], F32)
        ident = sb("ident", [P, P], F32)
        b1s = sb("b1s", [P, 4 * DC], F32)
        gam = sb("gam", [P, DC], F32)
        bet = sb("bet", [P, DC], F32)
        l1g = sb("l1g", [P, DC], F32)
        l1b = sb("l1b", [P, DC], F32)
        l2g = sb("l2g", [P, HC], F32)
        l2b = sb("l2b", [P, HC], F32)
        epst = sb("epst", [P, 2 * T], F32)
        mhalf = sb("mhalf", [P, 2 * T], F32)
        st1 = sb("st1", [P, T, 6], F32)
        mv1 = sb("mv1", [P, T, 2], F32)
        rp1 = sb("rp1", [P, 2 * T], F32)
        rs1 = sb("rs1", [P, 2 * T], F32)
        st2 = sb("st2", [P, 2, 2, 6], F32)
        mv2 = sb("mv2", [P, 2, 2], F32)
        rp2 = sb("rp2", [P, 2], F32)
        rs2 = sb("rs2", [P, 2], F32)
        st3 = sb("st3", [P, 2, 6], F32)
        mv3 = sb("mv3", [P, T, 2], F32)
        rp3 = sb("rp3", [P, 2], F32)
        rs3 = sb("rs3", [P, T], F32)
        asum = sb("asum", [P, 2], F32)
        cm = sb("cm", [P, 2], F32)
        scl = sb("scl", [P, 2], F32)
        cq = sb("cq", [P, 2], F32)
        w1raw = at("w1raw", [P, DC, 4 * D], F32, attn_at)
        wfraw = at("wfraw", [P, DC, HID], F32, attn_at + 4 * DC * 4 * D)
        wsraw = at("wsraw", [P, HC, D], F32, xh_at)
        bcasts = at("bcasts", [P, DC + HC, P], F32, xh_at + 4 * HC * D)
        ones = at("ones", [P, P], F32, xh_at + 4 * HC * D + 4 * (DC + HC) * P)
        onesm = at("onesm", [P, P], F32, xh_at + 4 * HC * D + 4 * (DC + HC + 1) * P)
        junk = at("junk", [P, HC * D], F32, part_at)
        w2raw, w2g = qkf, tmp
        b2b, fb2b = normed[:, 0, :], normed[:, 1, :]

        SP = ctx.enter_context(nc.psum_tensor("scores", [P, 4, HALF], F32))
        OP = ctx.enter_context(nc.psum_tensor("outs", [P, 2, HALF], F32))
        FP = ctx.enter_context(nc.psum_tensor("fill", [P, 2, HALF], F32))

        def sem(name):
            return ctx.enter_context(nc.semaphore(name))

        s_w1 = sem("w1_loaded")
        s_wf = sem("wf_loaded")
        s_ws = sem("ws_loaded")
        s_vec = sem("vectors_loaded")
        s_abs = sem("abs_summed")
        s_tot = sem("abs_total")
        s_const = sem("pool_constants")
        s_ones = sem("ones_made")
        s_bc = sem("setup_operands")
        s_cmm = sem("setup_products")
        s_setup = sem("setup_done")
        s_x = sem("x_loaded")
        s_norm = sem("normed_pair")
        s_mv1, s_rs1 = sem("input_moments"), sem("input_rstd")
        s_mv2, s_rs2 = sem("hidden_moments"), sem("hidden_rstd")
        s_mv3, s_rs3 = sem("z_moments"), sem("z_rstd")
        s_fill = [sem("filled0"), sem("filled1")]
        s_evac = [sem("evacuated0"), sem("evacuated1")]
        s_xh = sem("x_high_part")
        s_split = sem("qk_split")
        s_kw = sem("k_parts_written")
        s_qw = sem("q_parts_written")
        s_stack = [sem("stacked0"), sem("stacked1")]
        s_v = sem("v_ready")
        s_score = sem("scores_ready")
        s_silu = sem("attn_ready")
        s_av = sem("av_done")
        s_z = sem("z_ready")
        s_ht = sem("h_split")
        s_gelu = sem("gelu_done")
        s_hn = sem("hidden_normed")
        s_hg = sem("hidden_split")
        s_out = sem("out_written")

        block = ctx.enter_context(nc.Block())

        def wait_filled(eng, b, step):
            eng.wait_ge(s_fill[bank_of(step)], turn_of(b, step))

        def wait_evacuated(eng, b, step):
            eng.wait_ge(s_evac[bank_of(step)], turn_of(b, step))

        def steps(g, first, last):
            for s in SLOTS[g]:
                if first and s[0] in POST or last and (is_next(s) or s == ("vs", 0)):
                    continue
                yield s

        PRO = [s for s in ORDER if is_next(s) or s == ("vs", 0)]
        EPI = [s for s in ORDER if s[0] in POST]

        @block.sync
        def _(sp):
            def load_x(b):
                sp.dma_start(xin[:, :, :], xv[b, :, :, :]).then_inc(s_x, 16)

            def write_parts(b, c):
                if c == 0:
                    sp.wait_ge(s_stack[0], 96 * b)
                    sp.wait_ge(s_stack[1], 96 * b)
                for h in range(NH):
                    cols = slice(h * HALF, (h + 1) * HALF)
                    n = 2 * (NH * c + h)
                    sp.wait_ge(s_split, 8 * b + n + 1)
                    for r in range(PARTS + 2):
                        sp.dma_start(kd[c][:, r * DH:(r + 1) * DH, cols], kst[:, r % PARTS, :]).then_inc(s_kw, 16)
                    sp.wait_ge(s_split, 8 * b + n + 2)
                    for r in range(PARTS):
                        sp.dma_start(qd[c][:, r * DH:(r + 1) * DH, cols], qst[:, r, :]).then_inc(s_qw, 16)

            def load_stack(b, c, reused):
                sp.wait_ge(s_kw, 320 * b + 160 * (c + 1))
                sp.wait_ge(s_qw, 192 * b + 96 * (c + 1))
                if reused:
                    sp.wait_ge(s_score, 2 * GROUPS * (b - 1) + 2 * PHASE * (c + 1))
                heads = slice(c * HPC, (c + 1) * HPC)
                for i, first in enumerate((1, 2, 0)):
                    rows = QROWS if i < 2 else P - 2 * QROWS
                    dst = slice(i * QROWS, i * QROWS + rows)
                    sp.dma_start(KS[dst, heads, :],
                                 kd[c][:, first * DH:first * DH + rows, :].rearrange("h r n -> r h n")).then_inc(s_stack[c], 16)
                    sp.dma_start(QS[dst, heads, :],
                                 qd[c][:, 0:rows, :].rearrange("h r n -> r h n")).then_inc(s_stack[c], 16)

            def store(b):
                for i in range(2):
                    wait_evacuated(sp, b + 1, ("a", 2 * i + 1))
                    ts = slice(i * T // 2, (i + 1) * T // 2)
                    sp.dma_start(ov[b, :, ts, :], part[:, ts, :]).then_inc(s_out, 16)

            def body(b, first=False, last=False):
                if not first:
                    store(b - 1)
                write_parts(b, 1)
                load_stack(b, 1, not first)
                if not last:
                    sp.wait_ge(s_norm, NP + 2 * NP * b + NP)
                    load_x(b + 1)
                    write_parts(b + 1, 0)
                    load_stack(b + 1, 0, True)

            sp.dma_start(wfraw[:, :, :], w1T.rearrange("(c p) n -> p c n", p=P)).then_inc(s_wf, 16)
            sp.dma_start(wsraw[:, :, :], w2T.rearrange("(c p) n -> p c n", p=P)).then_inc(s_ws, 16)
            sp.dma_start(w1raw[:, :, :], W1.rearrange("(c p) n -> p c n", p=P)).then_inc(s_w1, 16)
            sp.dma_start(w2raw[:, :].rearrange("p (c n) -> p c n", c=DC), W2.rearrange("(c p) n -> p c n", p=P)).then_inc(s_w1, 16)
            for dst, src in ((b1s, b1c), (gam, gamc), (bet, betc), (l1g, l1gc), (l1b, l1bc), (l2g, l2gc), (l2b, l2bc)):
                sp.dma_start(dst[:, :], src).then_inc(s_vec, 16)
            for dst, src in ((bvb[:, :], b1[D:2 * D]), (fb1b[:, :], fb1), (b2b, b2), (fb2b, fb2)):
                sp.dma_start(dst, src.partition_broadcast(P)).then_inc(s_vec, 16)
            load_x(0)
            sp.wait_ge(s_setup, 1)
            write_parts(0, 0)
            load_stack(0, 0, False)
            body(0, first=True)
            with sp.Fori(1, NB - 1) as b:
                body(b)
            body(NB - 1, last=True)
            store(NB - 1)
            sp.wait_ge(s_out, 32 * NB)

        @block.gpsimd
        def _(pool):
            nc.gpsimd.memset(ident[:, :], 0.0)
            nc.gpsimd.memset(epst[:, :], EPS).then_inc(s_const, 1)
            nc.gpsimd.memset(mhalf[:, :], -0.5).then_inc(s_const, 1)
            nc.gpsimd.memset(V[:, :, :, :], 0.0).then_inc(s_const, 1)
            pool.drain()
            nc.gpsimd.affine_select(out=ident[:, :], in_=ident[:, :], compare_op=ALU.not_equal, fill=1.0,
                                    base=0, pattern=[[-1, P]], channel_multiplier=1).then_inc(s_const, 1)
            pool.wait_ge(s_const, 4)

            def rsqrt(out_ap, in_ap, tmp_ap, n, done):
                nc.gpsimd.tensor_tensor(tmp_ap, in_ap, epst[:, 0:n], ALU.add)
                pool.drain()
                nc.gpsimd.tensor_tensor(out_ap, tmp_ap, mhalf[:, 0:n], ALU.pow).then_inc(done, 1)

            def input_rstd(b):
                pool.wait_ge(s_mv1, b + 1)
                nc.gpsimd.tensor_tensor(rp1[:, 0:T], mv1[:, :, 1], epst[:, 0:T], ALU.add)
                pool.drain()
                nc.gpsimd.tensor_tensor(rp1[:, T:2 * T], rp1[:, 0:T], epst[:, 0:T], ALU.mult)
                pool.drain()
                nc.gpsimd.tensor_tensor(rp1[:, T:2 * T], rp1[:, T:2 * T], mv1[:, :, 1], ALU.add)
                pool.drain()
                nc.gpsimd.tensor_tensor(rs1[:, :], rp1[:, :], mhalf[:, :], ALU.pow).then_inc(s_rs1, 1)

            def step(b, kind, *a):
                if kind in ("zt", "ln2", "ln1"):
                    pool.drain()
                if kind == "zt":
                    pool.wait_ge(s_mv3, NP * (b - 1) + a[0] + 1)
                    rsqrt(rs3[:, 2 * a[0]:2 * a[0] + 2], mv3[:, 2 * a[0]:2 * a[0] + 2, 1], rp3[:, :], 2, s_rs3)
                elif kind == "ln2":
                    pool.wait_ge(s_mv2, NP * b + a[0] + 1)
                    rsqrt(rs2[:, :], mv2[:, :, 1], rp2[:, :], 2, s_rs2)
                elif kind == "ln1":
                    input_rstd(b + 1)

            def body(b, first=False, last=False):
                for g in range(GROUPS):
                    for s in steps(g, first, last):
                        step(b, *s)

            step(-1, "ln1")
            body(0, first=True)
            with pool.Fori(1, NB - 1) as b:
                body(b)
            body(NB - 1, last=True)
            for s in EPI:
                step(NB, *s)

        @block.scalar
        def _(act):
            def silu_group(b, g, first):
                for hf in range(2):
                    act.wait_ge(s_score, 2 * GROUPS * b + 2 * g + hf + 1)
                    if hf == 0 and not (first and g < 2):
                        act.wait_ge(s_av, GROUPS * b + g - 1)
                    nc.scalar.activation(attn[:, g % 2, 2 * hf:2 * hf + 2, :], SP[:, 2 * hf:2 * hf + 2, :],
                                         ACT.Silu).then_inc(s_silu, 1)

            def project(b, step, out_ap, col):
                wait_filled(act, b, step)
                k = bank_of(step)
                nc.scalar.activation(out_ap, FP[:, k, :], ACT.Silu, bias=b1s[:, col:col + 1]).then_inc(s_evac[k], 1)

            def place_v(b, c, reused):
                wait_evacuated(act, b - 1, ("v", NP - 1))
                if reused:
                    act.wait_ge(s_av, GROUPS * (b - 1) + PHASE * (c + 1))
                pairs = slice(c * HPC // 2, (c + 1) * HPC // 2)
                src = vraw[:, :, c * P:(c + 1) * P].rearrange("p t (j o d) -> p t j o d", o=2, d=DH)
                for o in range(2):
                    ins = nc.scalar.activation(V[:, :, pairs, 2 * o * DH:2 * o * DH + DH], src[:, :, :, o, :], ACT.Silu)
                ins.then_inc(s_v, 1)

            def step(b, first, kind, *a):
                me = (kind, *a)
                if kind == "xt":
                    wait_filled(act, b, me)
                    k, i = bank_of(me), a[0]
                    nc.scalar.activation(xh[:, :, i * PAIR:(i + 1) * PAIR],
                                         FP[:, k, :].rearrange("p (c n) -> p c n", c=DC), ACT.Copy).then_inc(s_xh, 1)
                elif kind in ("k", "q"):
                    c, h = a
                    n = 2 * (NH * c + h) + (kind == "q")
                    act.wait_ge(s_split, 8 * (b + 1 - c) + n)
                    project(b, me, qkf[:, :], (3 if kind == "k" else 2) * DC + c)
                elif kind == "u":
                    c, h = a
                    project(b, me, uz[:, c, h * HALF:(h + 1) * HALF], c)
                elif kind == "vs":
                    place_v(b if a[0] else b + 1, a[0], not (first and a[0] == 1))
                elif kind == "gelu":
                    i = a[0]
                    wait_evacuated(act, b, ("f1", 2 * i + 1, 1))
                    rows = hid[:, 2 * i % 4:2 * i % 4 + 2, :]
                    nc.scalar.activation(rows, rows, ACT.Gelu).then_inc(s_gelu, 1)

            def body(b, first=False, last=False):
                for g in range(GROUPS):
                    silu_group(b, g, first)
                    for s in steps(g, first, last):
                        step(b, first, *s)

            for i, (w, s) in enumerate(((wfraw, s_wf), (wsraw, s_ws))):
                act.wait_ge(s, 16)
                if i:
                    act.wait_ge(s_abs, i)
                nc.scalar.activation(junk[:, :], w[:, :, :].rearrange("p c n -> p (c n)"), ACT.Abs,
                                     accum_out=asum[:, i:i + 1]).then_inc(s_abs, 1)
            act.wait_ge(s_setup, 1)
            nc.scalar.preload_act_table(ACT.Silu)
            for s in PRO:
                if s[0] == "vs":
                    place_v(0, 0, False)
                else:
                    step(-1, True, *s)
            body(0, first=True)
            with act.Fori(1, NB - 1) as b:
                body(b)
            body(NB - 1, last=True)

        @block.vector
        def _(dve):
            V_ = nc.vector

            def setup():
                V_.memset(ones[:, :], 1.0).then_inc(s_ones, 1)
                V_.memset(onesm[:, :], 1.0 / D)
                dve.wait_ge(s_w1, 32)
                V_.tensor_copy(W1h[:, :, :], w1raw[:, :, :])
                dve.drain()
                V_.tensor_tensor(W1l[:, :, :], w1raw[:, :, :], W1h[:, :, :].bitcast(F32), ALU.subtract)
                dve.wait_ge(s_vec, 16 * 11)
                for c in range(DC):
                    cols = slice(c * D, (c + 1) * D)
                    V_.tensor_scalar(w2g[:, cols], w2raw[:, cols], gam[:, c:c + 1], None, ALU.mult)
                dve.wait_ge(s_ones, 1)
                for n in range(DC + HC):
                    v = bet[:, n:n + 1] if n < DC else l2b[:, n - DC:n - DC + 1]
                    ins = V_.tensor_scalar(bcasts[:, n, :], ones[:, :], v, None, ALU.mult)
                ins.then_inc(s_bc, 1)
                dve.wait_ge(s_tot, 1)
                V_.tensor_scalar(cm[:, :], FP[:, 0, 0:2], 1.0 / (D * HID), 1e-5, ALU.mult, ALU.max)
                dve.drain()
                V_.reciprocal(scl[:, :], cm[:, :])
                dve.drain()
                V_.reciprocal(cq[:, :], scl[:, :])
                for i, (raw, q) in enumerate(((wfraw, Wq1), (wsraw, Wq2))):
                    V_.tensor_scalar(raw[:, :, :], raw[:, :, :], scl[:, i:i + 1], 1.0, ALU.mult, ALU.min)
                    dve.drain()
                    V_.tensor_scalar(raw[:, :, :], raw[:, :, :], -1.0, ROUND, ALU.max, ALU.add)
                    dve.drain()
                    ins = V_.tensor_scalar(q[:, :, :], raw[:, :, :], ROUND, None, ALU.subtract)
                    ins.then_inc(s_bc, 1)
                dve.wait_ge(s_cmm, 1)
                for c in range(DC):
                    V_.tensor_tensor(W2c[:, c, :], w2g[:, c * D:(c + 1) * D], OP[:, 0, 0:D], ALU.subtract)
                V_.tensor_tensor(cst[:, :], OP[:, 1, 0:D], b2b, ALU.add)
                V_.scalar_tensor_tensor(out=junk[:, 0:D], in0=OP[:, 1, D:2 * D], scalar=cq[:, 1:2], in1=fb2b,
                                        op0=ALU.mult, op1=ALU.add)
                dve.drain()
                V_.tensor_tensor(cst[:, :], cst[:, :], junk[:, 0:D], ALU.add).then_inc(s_setup, 1)

            def stats(rows, st, mv, done):
                for j, views in enumerate(rows):
                    for n, v in enumerate(views):
                        V_.bn_stats(st[:, j, n, :] if len(views) > 1 else st[:, j, :], v)
                dve.drain()
                for j, views in enumerate(rows):
                    src = st[:, j, :, :].rearrange("p a b -> p (a b)") if len(views) > 1 else st[:, j, :]
                    ins = V_.bn_aggr(mv[:, j, :], src)
                ins.then_inc(done, 1)

            def norm_pair(b, i, col, after):
                if after is not None:
                    wait_filled(dve, *after)
                for j in range(2):
                    t = 2 * i + j
                    ins = V_.tensor_scalar(normed[:, j, :], xin[:, t, :], mv1[:, t, 0:1], rs1[:, col + t:col + t + 1],
                                           ALU.subtract, ALU.mult)
                ins.then_inc(s_norm, 1)

            def output(b, o):
                c, h = o // NH, o % NH
                dve.wait_ge(s_av, GROUPS * b + RUN * (o + 1))
                wait_evacuated(dve, b, ("u", c, h))
                z = uz[:, c, h * HALF:(h + 1) * HALF]
                V_.scalar_tensor_tensor(out=z, in0=OP[:, o % 2, :], scalar=1.0 / SEQ, in1=z,
                                        op0=ALU.mult, op1=ALU.mult).then_inc(s_z, 1)

            def step(b, kind, *a):
                dve.drain()
                me = (kind, *a)
                k = bank_of(me) if me in POS else None
                if kind == "zt":
                    i = a[0]
                    wait_filled(dve, b, me)
                    for j in range(2):
                        ins = V_.bn_stats(st3[:, j, :], FP[:, k, j * D:(j + 1) * D])
                    ins.then_inc(s_evac[k], 1)
                    dve.drain()
                    for j in range(2):
                        ins = V_.bn_aggr(mv3[:, 2 * i + j, :], st3[:, j, :])
                    ins.then_inc(s_mv3, 1)
                elif kind == "a":
                    i = a[0]
                    wait_filled(dve, b, me)
                    dve.wait_ge(s_rs3, NP * (b - 1) + i + 1)
                    for j in range(2):
                        t = 2 * i + j
                        ins = V_.scalar_tensor_tensor(out=part[:, t, :], in0=FP[:, k, j * D:(j + 1) * D],
                                                      scalar=rs3[:, t:t + 1], in1=part[:, t, :],
                                                      op0=ALU.mult, op1=ALU.add)
                    ins.then_inc(s_evac[k], 1)
                elif kind == "px":
                    dve.wait_ge(s_out, 32 * b)
                    V_.tensor_tensor(part[:, :, :], xin[:, :, :],
                                     cst[:, :].unsqueeze(1).broadcast_to([P, T, D]), ALU.add)
                elif kind == "hn":
                    i = a[0]
                    norm_pair(b, i, T, (b - 1, ("xt", NP - 1)) if i == 0 else (b, ("h", i - 1)))
                elif kind == "h":
                    wait_filled(dve, b, me)
                    y = tmp[:, :].rearrange("p (c n) -> p c n", c=DC)
                    for c in range(DC):
                        ins = V_.tensor_scalar(y[:, c, :], FP[:, k, c * PAIR:(c + 1) * PAIR],
                                               l1g[:, c:c + 1], l1b[:, c:c + 1], ALU.mult, ALU.add)
                    ins.then_inc(s_evac[k], 1)
                    dve.drain()
                    V_.tensor_copy(hTh[:, :, :], y)
                    dve.drain()
                    V_.tensor_tensor(hTl[:, :, :], y, hTh[:, :, :].bitcast(F32), ALU.subtract).then_inc(s_ht, 1)
                elif kind == "f1":
                    t, hf = a
                    wait_filled(dve, b, me)
                    cols = slice(hf * HALF, (hf + 1) * HALF)
                    V_.scalar_tensor_tensor(out=hid[:, t % 4, cols], in0=FP[:, k, :], scalar=cq[:, 0:1],
                                            in1=fb1b[:, cols], op0=ALU.mult, op1=ALU.add).then_inc(s_evac[k], 1)
                elif kind == "ln2":
                    i = a[0]
                    dve.wait_ge(s_gelu, NP * b + i + 1)
                    stats([[hid[:, (2 * i + j) % 4, n * HALF:(n + 1) * HALF] for n in range(2)] for j in range(2)],
                          st2, mv2, s_mv2)
                elif kind == "nrm2":
                    i = a[0]
                    dve.wait_ge(s_rs2, NP * b + i + 1)
                    for j in range(2):
                        row = hid[:, (2 * i + j) % 4, :]
                        ins = V_.tensor_scalar(row, row, mv2[:, j, 0:1], rs2[:, j:j + 1], ALU.subtract, ALU.mult)
                    ins.then_inc(s_hn, 1)
                elif kind == "g":
                    t, r = a
                    wait_filled(dve, b, me)
                    V_.tensor_tensor(tmp[:, :].rearrange("p (c n) -> p c n", n=P),
                                     FP[:, k, :].rearrange("p (c n) -> p c n", n=P),
                                     l2g[:, 4 * r:4 * r + 4].unsqueeze(2).broadcast_to([P, 4, P]),
                                     ALU.mult).then_inc(s_evac[k], 1)
                    dve.drain()
                    V_.tensor_copy(hgh[:, r, :], tmp[:, :])
                    dve.drain()
                    V_.tensor_tensor(hgl[:, r, :], tmp[:, :], hgh[:, r, :].bitcast(F32), ALU.subtract).then_inc(s_hg, 1)
                elif kind == "f2":
                    t = a[0]
                    wait_filled(dve, b, me)
                    V_.scalar_tensor_tensor(out=part[:, t, :], in0=FP[:, k, 0:D], scalar=cq[:, 1:2],
                                            in1=part[:, t, :], op0=ALU.mult, op1=ALU.add).then_inc(s_evac[k], 1)
                elif kind == "ln1":
                    dve.wait_ge(s_x, 16 * (b + 2))
                    stats([[xin[:, t, :]] for t in range(T)], st1, mv1, s_mv1)
                elif kind == "xn":
                    i = a[0]
                    if i == 0:
                        dve.wait_ge(s_rs1, b + 2)
                    prologue = isinstance(b, int) and b < 0
                    norm_pair(b, i, 0, (b, ("xt", i - 1)) if i else None if prologue else (b, ("h", NP - 1)))
                elif kind == "xt":
                    i = a[0]
                    dve.wait_ge(s_xh, NP * (b + 1) + i + 1)
                    cols = slice(i * PAIR, (i + 1) * PAIR)
                    V_.tensor_tensor(xl[:, :, cols], FP[:, k, :].rearrange("p (c n) -> p c n", c=DC),
                                     xh[:, :, cols].bitcast(F32), ALU.subtract).then_inc(s_evac[k], 1)
                elif kind in ("k", "q"):
                    c, h = a
                    dst, wrote, each = (kst, s_kw, 80) if kind == "k" else (qst, s_qw, 48)
                    wait_evacuated(dve, b, me)
                    dve.wait_ge(wrote, each * (4 * (b + 1 - c) + NH * c + h))
                    V_.tensor_copy(dst[:, 0, :], qkf[:, :])
                    dve.drain()
                    V_.tensor_tensor(qkf[:, :], qkf[:, :], dst[:, 0, :], ALU.subtract)
                    dve.drain()
                    V_.tensor_copy(dst[:, 1, :], qkf[:, :])
                    dve.drain()
                    V_.tensor_tensor(dst[:, 2, :], qkf[:, :], dst[:, 1, :], ALU.subtract).then_inc(s_split, 1)
                elif kind == "v":
                    i = a[0]
                    wait_filled(dve, b, me)
                    if i == 0:
                        dve.wait_ge(s_v, 2 * (b + 1))
                    V_.tensor_tensor(vraw[:, 2 * i:2 * i + 2, :], FP[:, k, :].rearrange("p (t n) -> p t n", t=2),
                                     bvb[:, :].unsqueeze(1).broadcast_to([P, 2, D]), ALU.add).then_inc(s_evac[k], 1)

            def body(b, first=False, last=False):
                for g in range(GROUPS):
                    for s in steps(g, first, last):
                        step(b, *s)
                    if g == 0 and not first:
                        output(b - 1, DC * NH - 1)
                    if g and g % RUN == 0:
                        output(b, g // RUN - 1)

            setup()
            for s in PRO:
                step(-1, *s)
            body(0, first=True)
            with dve.Fori(1, NB - 1) as b:
                body(b)
            body(NB - 1, last=True)
            output(NB - 1, DC * NH - 1)
            for s in EPI:
                step(NB, *s)

        @block.tensor
        def _(pe):
            mm = nc.tensor.matmul

            def where(g):
                return g // PHASE, g // RUN % NH, g // T % 2, g % T

            def scores(b, g, first):
                c, h, o, t = where(g)
                if g % PHASE == 0:
                    pe.wait_ge(s_stack[c], 96 * (b + 1))
                for j in range(4):
                    if j % 2 == 0 and not (first and g == 0):
                        pe.wait_ge(s_silu, 2 * GROUPS * b + 2 * g + j // 2 - 1)
                    head = c * HPC + 2 * j + o
                    ins = mm(SP[:, j, :], KS[:, head, t * P:(t + 1) * P], QS[:, head, h * HALF:(h + 1) * HALF],
                             start=True, stop=True)
                    if j % 2:
                        ins.then_inc(s_score, 1)

            def times_v(b, g, first):
                c, h, o, t = where(g)
                if g % PHASE == 0:
                    pe.wait_ge(s_v, 2 * b + c + 1)
                if g % RUN == 0 and not (first and g < 2 * RUN):
                    pe.wait_ge(s_z, DC * NH * b + g // RUN - 1)
                pe.wait_ge(s_silu, 2 * GROUPS * b + 2 * g + 2)
                for j in range(4):
                    ins = mm(OP[32 * j:32 * j + 32, g // RUN % 2, :], V[:, t, c * HPC // 2 + j, o * DH:o * DH + 2 * DH],
                             attn[:, g % 2, j, :], start=(o == 0 and t == 0), stop=(o == 1 and t == T - 1))
                ins.then_inc(s_av, 1)

            def weights(w, kc, col):
                return w[:, kc, col:col + P]

            def step(b, kind, *a):
                me = (kind, *a)
                if me not in POS:
                    return
                k = bank_of(me)
                bank = FP[:, k, :]
                if not (isinstance(b, int) and turn_of(b, me) <= 1):
                    pe.wait_ge(s_evac[k], turn_of(b, me) - 1)
                if kind in ("xt", "h"):
                    i = a[0]
                    pe.wait_ge(s_norm, (NP + 2 * NP * b + i + 1) if kind == "h" else (2 * NP * (b + 1) + i + 1))
                    for c in range(DC):
                        for j in range(2):
                            ins = nc.tensor.transpose(bank[:, c * PAIR + j * P:c * PAIR + (j + 1) * P],
                                                      normed[:, j, c * P:(c + 1) * P], ident[:, :])
                elif kind in ("k", "q", "u"):
                    c, h = a
                    wait_evacuated(pe, b if is_next(me) else b - 1, ("xt", 2 * h + 1))
                    col = {"u": 0, "q": 2 * D, "k": 3 * D}[kind] + c * P
                    cols = slice(h * HALF, (h + 1) * HALF)
                    passes = [(w, r, kc) for kc in range(DC) for w, r in ((W1h, xh), (W1h, xl), (W1l, xh))]
                    for n, (w, r, kc) in enumerate(passes):
                        ins = mm(bank, w[:, kc, col:col + P], r[:, kc, cols], start=n == 0, stop=n == len(passes) - 1)
                elif kind == "v":
                    i = a[0]
                    wait_evacuated(pe, b, ("xt", i))
                    passes = [(w, r, kc) for kc in range(DC) for w, r in ((W1h, xh), (W1h, xl), (W1l, xh))]
                    for j in range(2):
                        toks = slice((2 * i + j) * P, (2 * i + j + 1) * P)
                        for n, (w, r, kc) in enumerate(passes):
                            ins = mm(bank[:, j * D:(j + 1) * D], r[:, kc, toks], w[:, kc, D:2 * D],
                                     start=n == 0, stop=n == len(passes) - 1)
                elif kind == "f1":
                    t, hf = a
                    pe.wait_ge(s_ht, NP * b + t // 2 + 1)
                    passes = [(r, kc) for kc in range(DC) for r in (hTh, hTl)]
                    for n, (r, kc) in enumerate(passes):
                        ins = mm(bank, r[:, kc, t % 2 * P:(t % 2 + 1) * P], Wq1[:, kc, hf * HALF:(hf + 1) * HALF],
                                 start=n == 0, stop=n == len(passes) - 1)
                elif kind == "g":
                    t, r = a
                    pe.wait_ge(s_hn, NP * b + t // 2 + 1)
                    for n in range(4):
                        col = (4 * r + n) * P
                        ins = nc.tensor.transpose(bank[:, n * P:(n + 1) * P], hid[:, t % 4, col:col + P], ident[:, :])
                elif kind == "f2":
                    t = a[0]
                    passes = [(w, r, n) for r in range(2) for n in range(4) for w in (hgh, hgl)]
                    for i, (w, r, n) in enumerate(passes):
                        if i % 8 == 0:
                            pe.wait_ge(s_hg, 2 * T * b + 2 * t + r + 1)
                        ins = mm(bank[:, 0:D], w[:, r, n * P:(n + 1) * P], Wq2[:, 4 * r + n, :],
                                 start=i == 0, stop=i == len(passes) - 1)
                elif kind == "zt":
                    i = a[0]
                    if i == 0:
                        pe.wait_ge(s_z, DC * NH * b)
                    for j in range(2):
                        for c in range(DC):
                            toks = slice((2 * i + j) * P, (2 * i + j + 1) * P)
                            ins = nc.tensor.transpose(bank[:, j * D + c * P:j * D + (c + 1) * P], uz[:, c, toks], ident[:, :])
                elif kind == "a":
                    i = a[0]
                    for j in range(2):
                        toks = slice((2 * i + j) * P, (2 * i + j + 1) * P)
                        for c in range(DC):
                            ins = mm(bank[:, j * D:(j + 1) * D], uz[:, c, toks], W2c[:, c, :], start=c == 0, stop=c == DC - 1)
                ins.then_inc(s_fill[k], 1)

            def body(b, first=False, last=False):
                for g in range(GROUPS):
                    scores(b, g, first)
                    if g == 0 and not first:
                        times_v(b - 1, GROUPS - 1, False)
                    for s in steps(g, first, last):
                        step(b, *s)
                    if g:
                        times_v(b, g - 1, first)

            pe.wait_ge(s_abs, 2)
            pe.wait_ge(s_ones, 1)
            mm(FP[:, 0, 0:2], ones[:, :], asum[:, :], start=True, stop=True).then_inc(s_tot, 1)
            pe.wait_ge(s_bc, 3)
            for c in range(DC):
                mm(OP[:, 0, 0:D], onesm[:, :], w2g[:, c * D:(c + 1) * D], start=c == 0, stop=c == DC - 1)
            for c in range(DC):
                mm(OP[:, 1, 0:D], bcasts[:, c, :], w2raw[:, c * D:(c + 1) * D], start=c == 0, stop=c == DC - 1)
            for c in range(HC):
                ins = mm(OP[:, 1, D:2 * D], bcasts[:, DC + c, :], Wq2[:, c, :].bitcast(F32), start=c == 0, stop=c == HC - 1)
            ins.then_inc(s_cmm, 1)
            pe.wait_ge(s_setup, 1)
            pe.wait_ge(s_const, 4)
            for s in PRO:
                step(-1, *s)
            body(0, first=True)
            with pe.Fori(1, NB - 1) as b:
                body(b)
            body(NB - 1, last=True)
            times_v(NB - 1, GROUPS - 1, False)
            for s in EPI:
                step(NB, *s)



def kernel(L0_attn_x, L0_attn_W1, L0_attn_b1, L0_attn_W2, L0_attn_b2, L0_attn_gamma, L0_attn_beta,
           L0_ffn_ln1_g, L0_ffn_ln1_b, L0_ffn_w1, L0_ffn_b1, L0_ffn_ln2_g, L0_ffn_ln2_b, L0_ffn_w2, L0_ffn_b2):
    import numpy as _np
    import concourse.bacc as _bacc
    from concourse import mybir as _mybir
    from concourse.bass_utils import run_bass_kernel_spmd as _run

    def columns(v):
        return _np.ascontiguousarray(_np.asarray(v).reshape(-1, P).T)

    arrays = {
        "x": _np.ascontiguousarray(L0_attn_x),
        "W1": _np.ascontiguousarray(L0_attn_W1),
        "b1": _np.ascontiguousarray(L0_attn_b1),
        "b1c": columns(L0_attn_b1),
        "W2": _np.ascontiguousarray(L0_attn_W2),
        "b2": _np.ascontiguousarray(L0_attn_b2),
        "gamc": columns(L0_attn_gamma),
        "betc": columns(L0_attn_beta),
        "l1gc": columns(L0_ffn_ln1_g),
        "l1bc": columns(L0_ffn_ln1_b),
        "w1T": _np.ascontiguousarray(_np.asarray(L0_ffn_w1).T),
        "fb1": _np.ascontiguousarray(L0_ffn_b1),
        "l2gc": columns(L0_ffn_ln2_g),
        "l2bc": columns(L0_ffn_ln2_b),
        "w2T": _np.ascontiguousarray(_np.asarray(L0_ffn_w2).T),
        "fb2": _np.ascontiguousarray(L0_ffn_b2),
    }
    nc = _bacc.Bacc("TRN2", target_bir_lowering=False, num_devices=1)
    args = [nc.dram_tensor(f"in_{n}", a.shape, _mybir.dt.from_np(a.dtype), kind="ExternalInput").ap()
            for n, a in arrays.items()]
    out = nc.dram_tensor("out_dram", (NB, SEQ, D), _mybir.dt.float32, kind="ExternalOutput").ap()
    hybrid_block_kernel(nc, *args, out)
    r = _run(nc, [{f"in_{n}": a for n, a in arrays.items()}], core_ids=[0])
    return r.results[0]["out_dram"]
```

```python
import numpy as np

import concourse.bass as bass
from concourse import mybir
from contextlib import ExitStack

F32 = mybir.dt.float32
F32R = mybir.dt.float32r
BF16 = mybir.dt.bfloat16
ALU = mybir.AluOpType
ACT = mybir.ActivationFunctionType

P = 128
NB, SEQ, D = 8, 1024, 256
HEADS, DH = 16, 16
HID = 1024
EPS = 1e-5
DC = D // P
HC = HID // P
T = SEQ // P
HPC = P // DH
HALF = 512
NH = SEQ // HALF
PAIR = 2 * P
NP = T // 2
PARTS = 3
QROWS = PARTS * DH
KROWS = (PARTS + 2) * DH
GROUPS = DC * NH * 2 * T
PHASE = GROUPS // DC
RUN = 2 * T
ROUND = 1.5 * 2.0 ** 23

TABLE = (
    "zt.0",
    "zt.1",
    "zt.2",
    "a.0 vs.1",
    "zt.3",
    "a.1 a.2 a.3",
    "k.1.0 hn.0",
    "u.1.0 u.0.0 q.1.0",
    "k.1.1",
    "h.0 q.1.1",
    "u.1.1 px",
    "u.0.1",
    "hn.1 f1.0.0",
    "",
    "f1.0.1",
    "f1.1.0 f1.1.1 gelu.0 h.1",
    "f1.2.0 f1.2.1",
    "ln2.0 f1.3.0",
    "",
    "nrm2.0",
    "hn.2 f1.3.1 h.2",
    "g.0.0",
    "g.0.1",
    "f2.0",
    "hn.3 g.1.0",
    "g.1.1 gelu.1 f1.4.0 f1.4.1 ln2.1",
    "f2.1 f1.5.0",
    "nrm2.1 f1.5.1",
    "h.3",
    "g.2.0",
    "g.2.1",
    "f2.2 g.3.0",
    "g.3.1",
    "f1.6.0 gelu.2 f1.6.1",
    "f1.7.0 f2.3 f1.7.1",
    "",
    "ln2.2",
    "",
    "ln1 nrm2.2",
    "g.4.0",
    "g.4.1",
    "f2.4 g.5.0 gelu.3 g.5.1",
    "ln2.3 f2.5",
    "nrm2.3 xn.0",
    "",
    "g.6.0",
    "g.6.1",
    "f2.6",
    "g.7.0",
    "g.7.1",
    "xn.1 f2.7 xt.0 xn.2",
    "xt.1 xn.3",
    "xt.2 k.0.0",
    "xt.3 q.0.0",
    "k.0.1",
    "q.0.1",
    "v.0",
    "",
    "",
    "",
    "",
    "v.1",
    "v.2 v.3 vs.0",
    "",
)
SLOTS = [[(n.split(".")[0], *map(int, n.split(".")[1:])) for n in row.split()] for row in TABLE]
assert len(SLOTS) == GROUPS

POST = ("zt", "a")



def is_next(s):
    return s[0] in ("ln1", "xn", "xt", "v") or s[0] in ("k", "q") and s[1] == 0


FILLERS = ("zt", "a", "u", "h", "f1", "g", "f2", "xt", "k", "q", "v")
ORDER = [s for g in range(GROUPS) for s in SLOTS[g]]
PIECES = [s for s in ORDER if s[0] in FILLERS]
POS = {s: n for n, s in enumerate(PIECES)}
NPOST = sum(s[0] in POST for s in PIECES)
NNEXT = sum(is_next(s) for s in PIECES)
NPIECES = len(PIECES)
assert NPIECES % 2 == 0 and NPOST % 2 == 0 and NNEXT % 2 == 0
assert all(POS[s] < NPOST for s in PIECES if s[0] in POST)
assert all(POS[s] >= NPIECES - NNEXT for s in PIECES if is_next(s))


def bank_of(step):
    return POS[step] % 2


def turn_of(body, step):
    n = POS[step] // 2 + 1
    if isinstance(body, int) and body < 0:
        return n - (NPIECES - NNEXT) // 2
    base = body * (NPIECES // 2) + (NNEXT - NPOST) // 2
    if isinstance(body, int) and body == NB:
        base = base - NNEXT // 2
    return base + n


def hybrid_block_kernel(nc, x, W1, b1, b1c, W2, b2, gamc, betc, l1gc, l1bc, w1T, fb1, l2gc, l2bc, w2T, fb2, out):
    xv = x.rearrange("b (p t) d -> b p t d", p=P)
    ov = out.rearrange("b (p t) d -> b p t d", p=P)
    kd = [nc.dram_tensor(f"k_scratch{c}", [HPC, KROWS, SEQ], BF16, kind="Internal").ap() for c in range(DC)]
    qd = [nc.dram_tensor(f"q_scratch{c}", [HPC, QROWS, SEQ], BF16, kind="Internal").ap() for c in range(DC)]

    ctx = ExitStack()
    with ctx:
        top = [nc.sbuf_base + (-nc.sbuf_base) % 64]

        def at(name, shape, dt, offset):
            return nc.alloc_sbuf_tensor_at(name, shape, dt, offset=offset)

        def sb(name, shape, dt):
            offset = top[0]
            size = int(np.prod(shape[1:])) * (2 if dt == BF16 else 4)
            top[0] = offset + size + (-size) % 32
            return at(name, shape, dt, offset)

        qs_at = top[0]
        QS = sb("QS", [P, HEADS, SEQ], BF16)
        KS = sb("KS", [P, HEADS, SEQ], BF16)
        V = sb("V", [P, T, HEADS // 2, 3 * DH], F32)
        uz_at = top[0]
        uz = sb("uz", [P, DC, SEQ], F32)
        attn_at = top[0]
        attn = sb("attn", [P, 2, 4, HALF], F32)
        W1h = sb("W1h", [P, DC, 4 * D], F32R)
        W1l = sb("W1l", [P, DC, 4 * D], F32R)
        Wq1 = sb("Wq1", [P, DC, HID], F32R)
        Wq2 = sb("Wq2", [P, HC, D], F32R)
        W2c = sb("W2c", [P, DC, D], F32)
        vraw = sb("vraw", [P, T, D], F32)
        xh_at = top[0]
        xh = sb("xh", [P, DC, SEQ], F32R)
        xl = sb("xl", [P, DC, SEQ], F32R)
        hid = at("hid", [P, 4, HID], F32, xh_at)
        hT_at = top[0]
        hTh = sb("hTh", [P, DC, PAIR], F32R)
        hTl = sb("hTl", [P, DC, PAIR], F32R)
        hgh = sb("hgh", [P, 2, HALF], F32R)
        hgl = sb("hgl", [P, 2, HALF], F32R)
        part_at = top[0]
        part = sb("part", [P, T, D], F32)
        xin = sb("xin", [P, T, D], F32)
        fb1b = sb("fb1b", [P, HID], F32)
        kst = sb("kst", [P, PARTS, HALF], BF16)
        qst = sb("qst", [P, PARTS, HALF], BF16)
        qkf = sb("qkf", [P, HALF], F32)
        normed = sb("normed", [P, 2, D], F32)
        tmp = sb("tmp", [P, HALF], F32)
        bvb = sb("bvb", [P, D], F32)
        cst = sb("cst", [P, D], F32)
        ident = sb("ident", [P, P], F32)
        b1s = sb("b1s", [P, 4 * DC], F32)
        gam = sb("gam", [P, DC], F32)
        bet = sb("bet", [P, DC], F32)
        l1g = sb("l1g", [P, DC], F32)
        l1b = sb("l1b", [P, DC], F32)
        l2g = sb("l2g", [P, HC], F32)
        l2b = sb("l2b", [P, HC], F32)
        epst = sb("epst", [P, 2 * T], F32)
        mhalf = sb("mhalf", [P, 2 * T], F32)
        st1 = sb("st1", [P, T, 6], F32)
        mv1 = sb("mv1", [P, T, 2], F32)
        rp1 = sb("rp1", [P, 2 * T], F32)
        rs1 = sb("rs1", [P, 2 * T], F32)
        st2 = sb("st2", [P, 2, 2, 6], F32)
        mv2 = sb("mv2", [P, 2, 2], F32)
        rp2 = sb("rp2", [P, 2], F32)
        rs2 = sb("rs2", [P, 2], F32)
        st3 = sb("st3", [P, 2, 6], F32)
        mv3 = sb("mv3", [P, T, 2], F32)
        rp3 = sb("rp3", [P, 2], F32)
        rs3 = sb("rs3", [P, T], F32)
        asum = sb("asum", [P, 2], F32)
        cm = sb("cm", [P, 2], F32)
        scl = sb("scl", [P, 2], F32)
        cq = sb("cq", [P, 2], F32)
        w1raw = at("w1raw", [P, DC, 4 * D], F32, attn_at)
        wfraw = at("wfraw", [P, DC, HID], F32, qs_at + 2 * HPC * SEQ)
        wsraw = at("wsraw", [P, HC, D], F32, qs_at + 2 * HPC * SEQ + 4 * DC * HID)
        w2raw = at("w2raw", [P, DC * D], F32, hT_at)
        b2b = at("b2b", [P, D], F32, hT_at + 4 * DC * D)
        fb2b = at("fb2b", [P, D], F32, hT_at + 4 * (DC + 1) * D)
        bcasts = at("bcasts", [P, DC + HC, P], F32, uz_at)
        ones = at("ones", [P, P], F32, uz_at + 4 * (DC + HC) * P)
        onesm = at("onesm", [P, P], F32, uz_at + 4 * (DC + HC + 1) * P)
        junk = at("junk", [P, HC * D], F32, part_at)
        w2g = tmp

        SP = ctx.enter_context(nc.psum_tensor("scores", [P, 4, HALF], F32))
        OP = ctx.enter_context(nc.psum_tensor("outs", [P, 2, HALF], F32))
        FP = ctx.enter_context(nc.psum_tensor("fill", [P, 2, HALF], F32))

        def sem(name):
            return ctx.enter_context(nc.semaphore(name))

        s_w1 = sem("w1_loaded")
        s_w1s = sem("w1_split")
        s_b1 = sem("projection_biases_loaded")
        s_wf = sem("wf_loaded")
        s_ws = sem("ws_loaded")
        s_vec = sem("vectors_loaded")
        s_abs = sem("abs_summed")
        s_tot = sem("abs_total")
        s_ident = sem("identity_made")
        s_const = sem("pool_constants")
        s_ones = sem("ones_made")
        s_bc = sem("setup_operands")
        s_scl = sem("ternary_scales")
        s_tern = sem("ternary_weights")
        s_cmm = sem("setup_products")
        s_setup = sem("setup_done")
        s_x = sem("x_loaded")
        s_norm = sem("normed_pair")
        s_mv1, s_rs1 = sem("input_moments"), sem("input_rstd")
        s_mv2, s_rs2 = sem("hidden_moments"), sem("hidden_rstd")
        s_mv3, s_rs3 = sem("z_moments"), sem("z_rstd")
        s_fill = [sem("filled0"), sem("filled1")]
        s_evac = [sem("evacuated0"), sem("evacuated1")]
        s_xh = sem("x_high_part")
        s_split = sem("qk_split")
        s_kw = sem("k_parts_written")
        s_qw = sem("q_parts_written")
        s_stack = [[sem(f"stacked{c}_{h}") for h in range(NH)] for c in range(DC)]
        s_v = sem("v_ready")
        s_score = sem("scores_ready")
        s_silu = sem("attn_ready")
        s_av = sem("av_done")
        s_z = sem("z_ready")
        s_ht = sem("h_split")
        s_gelu = sem("gelu_done")
        s_hn = sem("hidden_normed")
        s_hg = sem("hidden_split")
        s_out = sem("out_written")

        block = ctx.enter_context(nc.Block())

        def wait_filled(eng, b, step):
            eng.wait_ge(s_fill[bank_of(step)], turn_of(b, step))

        def wait_evacuated(eng, b, step):
            eng.wait_ge(s_evac[bank_of(step)], turn_of(b, step))

        def steps(g, first, last):
            for s in SLOTS[g]:
                if first and s[0] in POST or last and (is_next(s) or s == ("vs", 0)):
                    continue
                yield s

        PRO = [s for s in ORDER if is_next(s) or s == ("vs", 0)]
        EPI = [s for s in ORDER if s[0] in POST]

        @block.sync
        def _(sp):
            def load_x(b):
                sp.dma_start(xin[:, :, :], xv[b, :, :, :]).then_inc(s_x, 16)

            def write_parts(b, c, h):
                if c == 0 and h == 0:
                    for cc in range(DC):
                        for hh in range(NH):
                            sp.wait_ge(s_stack[cc][hh], 96 * b)
                cols = slice(h * HALF, (h + 1) * HALF)
                n = 2 * (NH * c + h)
                sp.wait_ge(s_split, 8 * b + n + 1)
                for r in range(PARTS + 2):
                    sp.dma_start(kd[c][:, r * DH:(r + 1) * DH, cols], kst[:, r % PARTS, :]).then_inc(s_kw, 16)
                sp.wait_ge(s_split, 8 * b + n + 2)
                for r in range(PARTS):
                    sp.dma_start(qd[c][:, r * DH:(r + 1) * DH, cols], qst[:, r, :]).then_inc(s_qw, 16)

            def load_stack(b, c, h, reused):
                sp.wait_ge(s_kw, 320 * b + 80 * (NH * c + h + 1))
                sp.wait_ge(s_qw, 48 * (4 * b + NH * c + h + 1))
                if reused:
                    sp.wait_ge(s_score, 2 * GROUPS * (b - 1) + 2 * PHASE * (c + 1))
                heads = slice(c * HPC, (c + 1) * HPC)
                cols = slice(h * HALF, (h + 1) * HALF)
                for i, first in enumerate((1, 2, 0)):
                    rows = QROWS if i < 2 else P - 2 * QROWS
                    dst = slice(i * QROWS, i * QROWS + rows)
                    sp.dma_start(KS[dst, heads, cols],
                                 kd[c][:, first * DH:first * DH + rows, cols].rearrange("h r n -> r h n")).then_inc(s_stack[c][h], 16)
                    sp.dma_start(QS[dst, heads, cols],
                                 qd[c][:, 0:rows, cols].rearrange("h r n -> r h n")).then_inc(s_stack[c][h], 16)

            def store(b):
                for i in range(2):
                    wait_evacuated(sp, b + 1, ("a", 2 * i + 1))
                    ts = slice(i * T // 2, (i + 1) * T // 2)
                    sp.dma_start(ov[b, :, ts, :], part[:, ts, :]).then_inc(s_out, 16)

            def body(b, first=False, last=False):
                if not first:
                    store(b - 1)
                for h in range(NH):
                    write_parts(b, 1, h)
                    if first and h == 0:
                        sp.wait_ge(s_tern, 2)
                    load_stack(b, 1, h, not first)
                if not last:
                    sp.wait_ge(s_norm, NP + 2 * NP * b + NP)
                    load_x(b + 1)
                    for h in range(NH):
                        write_parts(b + 1, 0, h)
                        load_stack(b + 1, 0, h, True)

            load_x(0)
            sp.dma_start(w1raw[:, :, :], W1.rearrange("(c p) n -> p c n", p=P)).then_inc(s_w1, 16)
            sp.dma_start(b1s[:, :], b1c).then_inc(s_b1, 16)
            sp.dma_start(bvb[:, :], b1[D:2 * D].partition_broadcast(P)).then_inc(s_b1, 16)
            sp.dma_start(wfraw[:, :, :], w1T.rearrange("(c p) n -> p c n", p=P)).then_inc(s_wf, 16)
            sp.dma_start(wsraw[:, :, :], w2T.rearrange("(c p) n -> p c n", p=P)).then_inc(s_ws, 16)
            sp.dma_start(w2raw[:, :].rearrange("p (c n) -> p c n", c=DC), W2.rearrange("(c p) n -> p c n", p=P)).then_inc(s_vec, 16)
            for dst, src in ((gam, gamc), (bet, betc), (l1g, l1gc), (l1b, l1bc), (l2g, l2gc), (l2b, l2bc)):
                sp.dma_start(dst[:, :], src).then_inc(s_vec, 16)
            for dst, src in ((fb1b, fb1), (b2b, b2), (fb2b, fb2)):
                sp.dma_start(dst[:, :], src.partition_broadcast(P)).then_inc(s_vec, 16)
            for h in range(NH):
                write_parts(0, 0, h)
                load_stack(0, 0, h, False)
            body(0, first=True)
            with sp.Fori(1, NB - 1) as b:
                body(b)
            body(NB - 1, last=True)
            store(NB - 1)
            sp.wait_ge(s_out, 32 * NB)

        @block.gpsimd
        def _(pool):
            nc.gpsimd.memset(ident[:, :], 0.0)
            nc.gpsimd.memset(epst[:, :], EPS).then_inc(s_const, 1)
            nc.gpsimd.memset(mhalf[:, :], -0.5).then_inc(s_const, 1)
            pool.drain()
            nc.gpsimd.affine_select(out=ident[:, :], in_=ident[:, :], compare_op=ALU.not_equal, fill=1.0,
                                    base=0, pattern=[[-1, P]], channel_multiplier=1).then_inc(s_ident, 1)

            def rsqrt(out_ap, in_ap, tmp_ap, n, done):
                nc.gpsimd.tensor_tensor(tmp_ap, in_ap, epst[:, 0:n], ALU.add)
                pool.drain()
                nc.gpsimd.tensor_tensor(out_ap, tmp_ap, mhalf[:, 0:n], ALU.pow).then_inc(done, 1)

            def input_rstd(b):
                pool.wait_ge(s_mv1, b + 1)
                nc.gpsimd.tensor_tensor(rp1[:, 0:T], mv1[:, :, 1], epst[:, 0:T], ALU.add)
                pool.drain()
                nc.gpsimd.tensor_tensor(rp1[:, T:2 * T], rp1[:, 0:T], epst[:, 0:T], ALU.mult)
                pool.drain()
                nc.gpsimd.tensor_tensor(rp1[:, T:2 * T], rp1[:, T:2 * T], mv1[:, :, 1], ALU.add)
                pool.drain()
                nc.gpsimd.tensor_tensor(rs1[:, :], rp1[:, :], mhalf[:, :], ALU.pow).then_inc(s_rs1, 1)

            def step(b, kind, *a):
                if kind in ("zt", "ln2", "ln1"):
                    pool.drain()
                if kind == "zt":
                    pool.wait_ge(s_mv3, NP * (b - 1) + a[0] + 1)
                    rsqrt(rs3[:, 2 * a[0]:2 * a[0] + 2], mv3[:, 2 * a[0]:2 * a[0] + 2, 1], rp3[:, :], 2, s_rs3)
                elif kind == "ln2":
                    pool.wait_ge(s_mv2, NP * b + a[0] + 1)
                    rsqrt(rs2[:, :], mv2[:, :, 1], rp2[:, :], 2, s_rs2)
                elif kind == "ln1":
                    input_rstd(b + 1)

            def body(b, first=False, last=False):
                for g in range(GROUPS):
                    for s in steps(g, first, last):
                        step(b, *s)

            pool.wait_ge(s_const, 2)
            step(-1, "ln1")
            nc.gpsimd.memset(V[:, :, :, :], 0.0).then_inc(s_const, 1)
            body(0, first=True)
            with pool.Fori(1, NB - 1) as b:
                body(b)
            body(NB - 1, last=True)
            for s in EPI:
                step(NB, *s)

        @block.scalar
        def _(act):
            def silu_group(b, g, first):
                for hf in range(2):
                    act.wait_ge(s_score, 2 * GROUPS * b + 2 * g + hf + 1)
                    if hf == 0 and not (first and g < 2):
                        act.wait_ge(s_av, GROUPS * b + g - 1)
                    nc.scalar.activation(attn[:, g % 2, 2 * hf:2 * hf + 2, :], SP[:, 2 * hf:2 * hf + 2, :],
                                         ACT.Silu).then_inc(s_silu, 1)

            def project(b, step, out_ap, col):
                wait_filled(act, b, step)
                k = bank_of(step)
                nc.scalar.activation(out_ap, FP[:, k, :], ACT.Silu, bias=b1s[:, col:col + 1]).then_inc(s_evac[k], 1)

            def place_v(b, c, reused):
                wait_evacuated(act, b - 1, ("v", NP - 1))
                if reused:
                    act.wait_ge(s_av, GROUPS * (b - 1) + PHASE * (c + 1))
                pairs = slice(c * HPC // 2, (c + 1) * HPC // 2)
                src = vraw[:, :, c * P:(c + 1) * P].rearrange("p t (j o d) -> p t j o d", o=2, d=DH)
                for o in range(2):
                    ins = nc.scalar.activation(V[:, :, pairs, 2 * o * DH:2 * o * DH + DH], src[:, :, :, o, :], ACT.Silu)
                ins.then_inc(s_v, 1)

            def step(b, first, kind, *a):
                me = (kind, *a)
                if kind == "xt":
                    wait_filled(act, b, me)
                    k, i = bank_of(me), a[0]
                    nc.scalar.activation(xh[:, :, i * PAIR:(i + 1) * PAIR],
                                         FP[:, k, :].rearrange("p (c n) -> p c n", c=DC), ACT.Copy).then_inc(s_xh, 1)
                elif kind in ("k", "q"):
                    c, h = a
                    n = 2 * (NH * c + h) + (kind == "q")
                    act.wait_ge(s_split, 8 * (b + 1 - c) + n)
                    project(b, me, qkf[:, :], (3 if kind == "k" else 2) * DC + c)
                elif kind == "u":
                    c, h = a
                    project(b, me, uz[:, c, h * HALF:(h + 1) * HALF], c)
                elif kind == "vs":
                    place_v(b if a[0] else b + 1, a[0], not (first and a[0] == 1))
                elif kind == "gelu":
                    i = a[0]
                    wait_evacuated(act, b, ("f1", 2 * i + 1, 1))
                    rows = hid[:, 2 * i % 4:2 * i % 4 + 2, :]
                    nc.scalar.activation(rows, rows, ACT.Gelu).then_inc(s_gelu, 1)

            def body(b, first=False, last=False):
                for g in range(GROUPS):
                    silu_group(b, g, first)
                    for s in steps(g, first, last):
                        step(b, first, *s)

            def sum_of_abs(i):
                w, loaded = ((wfraw, s_wf), (wsraw, s_ws))[i]
                act.wait_ge(loaded, 16)
                if i:
                    act.wait_ge(s_abs, i)
                nc.scalar.activation(junk[:, :], w[:, :, :].rearrange("p c n -> p (c n)"), ACT.Abs,
                                     accum_out=asum[:, i:i + 1]).then_inc(s_abs, 1)

            nc.scalar.preload_act_table(ACT.Silu)
            act.wait_ge(s_b1, 32)
            for s in PRO:
                if s[0] == "vs":
                    act.wait_ge(s_const, 3)
                    place_v(0, 0, False)
                else:
                    step(-1, True, *s)
                if s[0] == "q":
                    sum_of_abs(s[2])
            body(0, first=True)
            with act.Fori(1, NB - 1) as b:
                body(b)
            body(NB - 1, last=True)

        @block.vector
        def _(dve):
            V_ = nc.vector

            def split_w1():
                dve.wait_ge(s_w1, 16)
                V_.tensor_copy(W1h[:, :, :], w1raw[:, :, :])
                dve.drain()
                V_.tensor_tensor(W1l[:, :, :], w1raw[:, :, :], W1h[:, :, :].bitcast(F32), ALU.subtract).then_inc(s_w1s, 1)

            def setup_broadcasts():
                V_.memset(onesm[:, :], 1.0 / D)
                dve.wait_ge(s_vec, 16 * 10)
                for c in range(DC):
                    cols = slice(c * D, (c + 1) * D)
                    V_.tensor_scalar(w2g[:, cols], w2raw[:, cols], gam[:, c:c + 1], None, ALU.mult)
                dve.wait_ge(s_ones, 1)
                for n in range(DC + HC):
                    v = bet[:, n:n + 1] if n < DC else l2b[:, n - DC:n - DC + 1]
                    ins = V_.tensor_scalar(bcasts[:, n, :], ones[:, :], v, None, ALU.mult)
                ins.then_inc(s_bc, 1)

            def setup_scales():
                dve.wait_ge(s_tot, 1)
                V_.tensor_scalar(cm[:, :], SP[:, 0, 0:2], 1.0 / (D * HID), 1e-5, ALU.mult, ALU.max)
                dve.drain()
                V_.reciprocal(scl[:, :], cm[:, :])
                dve.drain()
                V_.reciprocal(cq[:, :], scl[:, :]).then_inc(s_scl, 1)

            def setup_ternary(raw, q, scale):
                dve.drain()
                V_.tensor_scalar(raw[:, :, :], raw[:, :, :], scale, 1.0, ALU.mult, ALU.min)
                dve.drain()
                V_.tensor_scalar(raw[:, :, :], raw[:, :, :], -1.0, ROUND, ALU.max, ALU.add)
                dve.drain()
                V_.tensor_scalar(q[:, :, :], raw[:, :, :], ROUND, None, ALU.subtract).then_inc(s_tern, 1)

            def setup_w2():
                dve.wait_ge(s_cmm, 1)
                for c in range(DC):
                    V_.tensor_tensor(W2c[:, c, :], w2g[:, c * D:(c + 1) * D], FP[:, 0, 0:D], ALU.subtract)
                V_.tensor_tensor(cst[:, :], FP[:, 0, D:2 * D], b2b[:, :], ALU.add).then_inc(s_setup, 1)

            def setup_hidden():
                dve.drain()
                dve.wait_ge(s_cmm, 2)
                V_.scalar_tensor_tensor(out=junk[:, 0:D], in0=FP[:, 1, 0:D], scalar=cq[:, 1:2], in1=fb2b[:, :],
                                        op0=ALU.mult, op1=ALU.add).then_inc(s_setup, 1)
                dve.drain()
                V_.tensor_tensor(cst[:, :], cst[:, :], junk[:, 0:D], ALU.add)

            def stats(rows, st, mv, done):
                for j, views in enumerate(rows):
                    for n, v in enumerate(views):
                        V_.bn_stats(st[:, j, n, :] if len(views) > 1 else st[:, j, :], v)
                dve.drain()
                for j, views in enumerate(rows):
                    src = st[:, j, :, :].rearrange("p a b -> p (a b)") if len(views) > 1 else st[:, j, :]
                    ins = V_.bn_aggr(mv[:, j, :], src)
                ins.then_inc(done, 1)

            def norm_pair(b, i, col, after):
                if after is not None:
                    wait_filled(dve, *after)
                for j in range(2):
                    t = 2 * i + j
                    ins = V_.tensor_scalar(normed[:, j, :], xin[:, t, :], mv1[:, t, 0:1], rs1[:, col + t:col + t + 1],
                                           ALU.subtract, ALU.mult)
                ins.then_inc(s_norm, 1)

            def output(b, o):
                c, h = o // NH, o % NH
                dve.wait_ge(s_av, GROUPS * b + RUN * (o + 1))
                wait_evacuated(dve, b, ("u", c, h))
                z = uz[:, c, h * HALF:(h + 1) * HALF]
                V_.scalar_tensor_tensor(out=z, in0=OP[:, o % 2, :], scalar=1.0 / SEQ, in1=z,
                                        op0=ALU.mult, op1=ALU.mult).then_inc(s_z, 1)

            def step(b, kind, *a):
                dve.drain()
                me = (kind, *a)
                k = bank_of(me) if me in POS else None
                if kind == "zt":
                    i = a[0]
                    wait_filled(dve, b, me)
                    for j in range(2):
                        ins = V_.bn_stats(st3[:, j, :], FP[:, k, j * D:(j + 1) * D])
                    ins.then_inc(s_evac[k], 1)
                    dve.drain()
                    for j in range(2):
                        ins = V_.bn_aggr(mv3[:, 2 * i + j, :], st3[:, j, :])
                    ins.then_inc(s_mv3, 1)
                elif kind == "a":
                    i = a[0]
                    wait_filled(dve, b, me)
                    dve.wait_ge(s_rs3, NP * (b - 1) + i + 1)
                    for j in range(2):
                        t = 2 * i + j
                        ins = V_.scalar_tensor_tensor(out=part[:, t, :], in0=FP[:, k, j * D:(j + 1) * D],
                                                      scalar=rs3[:, t:t + 1], in1=part[:, t, :],
                                                      op0=ALU.mult, op1=ALU.add)
                    ins.then_inc(s_evac[k], 1)
                elif kind == "px":
                    dve.wait_ge(s_out, 32 * b)
                    V_.tensor_tensor(part[:, :, :], xin[:, :, :],
                                     cst[:, :].unsqueeze(1).broadcast_to([P, T, D]), ALU.add)
                elif kind == "hn":
                    i = a[0]
                    norm_pair(b, i, T, (b - 1, ("xt", NP - 1)) if i == 0 else (b, ("h", i - 1)))
                elif kind == "h":
                    wait_filled(dve, b, me)
                    y = tmp[:, :].rearrange("p (c n) -> p c n", c=DC)
                    for c in range(DC):
                        ins = V_.tensor_scalar(y[:, c, :], FP[:, k, c * PAIR:(c + 1) * PAIR],
                                               l1g[:, c:c + 1], l1b[:, c:c + 1], ALU.mult, ALU.add)
                    ins.then_inc(s_evac[k], 1)
                    dve.drain()
                    V_.tensor_copy(hTh[:, :, :], y)
                    dve.drain()
                    V_.tensor_tensor(hTl[:, :, :], y, hTh[:, :, :].bitcast(F32), ALU.subtract).then_inc(s_ht, 1)
                elif kind == "f1":
                    t, hf = a
                    wait_filled(dve, b, me)
                    cols = slice(hf * HALF, (hf + 1) * HALF)
                    V_.scalar_tensor_tensor(out=hid[:, t % 4, cols], in0=FP[:, k, :], scalar=cq[:, 0:1],
                                            in1=fb1b[:, cols], op0=ALU.mult, op1=ALU.add).then_inc(s_evac[k], 1)
                elif kind == "ln2":
                    i = a[0]
                    dve.wait_ge(s_gelu, NP * b + i + 1)
                    stats([[hid[:, (2 * i + j) % 4, n * HALF:(n + 1) * HALF] for n in range(2)] for j in range(2)],
                          st2, mv2, s_mv2)
                elif kind == "nrm2":
                    i = a[0]
                    dve.wait_ge(s_rs2, NP * b + i + 1)
                    for j in range(2):
                        row = hid[:, (2 * i + j) % 4, :]
                        ins = V_.tensor_scalar(row, row, mv2[:, j, 0:1], rs2[:, j:j + 1], ALU.subtract, ALU.mult)
                    ins.then_inc(s_hn, 1)
                elif kind == "g":
                    t, r = a
                    wait_filled(dve, b, me)
                    V_.tensor_tensor(tmp[:, :].rearrange("p (c n) -> p c n", n=P),
                                     FP[:, k, :].rearrange("p (c n) -> p c n", n=P),
                                     l2g[:, 4 * r:4 * r + 4].unsqueeze(2).broadcast_to([P, 4, P]),
                                     ALU.mult).then_inc(s_evac[k], 1)
                    dve.drain()
                    V_.tensor_copy(hgh[:, r, :], tmp[:, :])
                    dve.drain()
                    V_.tensor_tensor(hgl[:, r, :], tmp[:, :], hgh[:, r, :].bitcast(F32), ALU.subtract).then_inc(s_hg, 1)
                elif kind == "f2":
                    t = a[0]
                    wait_filled(dve, b, me)
                    V_.scalar_tensor_tensor(out=part[:, t, :], in0=FP[:, k, 0:D], scalar=cq[:, 1:2],
                                            in1=part[:, t, :], op0=ALU.mult, op1=ALU.add).then_inc(s_evac[k], 1)
                elif kind == "ln1":
                    dve.wait_ge(s_x, 16 * (b + 2))
                    stats([[xin[:, t, :]] for t in range(T)], st1, mv1, s_mv1)
                elif kind == "xn":
                    i = a[0]
                    if i == 0:
                        dve.wait_ge(s_rs1, b + 2)
                    prologue = isinstance(b, int) and b < 0
                    norm_pair(b, i, 0, (b, ("xt", i - 1)) if i else None if prologue else (b, ("h", NP - 1)))
                elif kind == "xt":
                    i = a[0]
                    dve.wait_ge(s_xh, NP * (b + 1) + i + 1)
                    cols = slice(i * PAIR, (i + 1) * PAIR)
                    V_.tensor_tensor(xl[:, :, cols], FP[:, k, :].rearrange("p (c n) -> p c n", c=DC),
                                     xh[:, :, cols].bitcast(F32), ALU.subtract).then_inc(s_evac[k], 1)
                elif kind in ("k", "q"):
                    c, h = a
                    dst, wrote, each = (kst, s_kw, 80) if kind == "k" else (qst, s_qw, 48)
                    wait_evacuated(dve, b, me)
                    dve.wait_ge(wrote, each * (4 * (b + 1 - c) + NH * c + h))
                    V_.tensor_copy(dst[:, 0, :], qkf[:, :])
                    dve.drain()
                    V_.tensor_tensor(qkf[:, :], qkf[:, :], dst[:, 0, :], ALU.subtract)
                    dve.drain()
                    V_.tensor_copy(dst[:, 1, :], qkf[:, :])
                    dve.drain()
                    V_.tensor_tensor(dst[:, 2, :], qkf[:, :], dst[:, 1, :], ALU.subtract).then_inc(s_split, 1)
                elif kind == "v":
                    i = a[0]
                    wait_filled(dve, b, me)
                    if i == 0:
                        dve.wait_ge(s_v, 2 * (b + 1))
                    V_.tensor_tensor(vraw[:, 2 * i:2 * i + 2, :], FP[:, k, :].rearrange("p (t n) -> p t n", t=2),
                                     bvb[:, :].unsqueeze(1).broadcast_to([P, 2, D]), ALU.add).then_inc(s_evac[k], 1)

            def setup_step(g):
                if g == 0:
                    dve.drain()
                    setup_broadcasts()
                    setup_ternary(wsraw, Wq2, scl[:, 1:2])
                elif g == 3:
                    setup_w2()
                    setup_ternary(wfraw, Wq1, scl[:, 0:1])
                elif g == 5:
                    setup_hidden()

            def body(b, first=False, last=False):
                for g in range(GROUPS):
                    if first:
                        setup_step(g)
                    for s in steps(g, first, last):
                        step(b, *s)
                    if g == 0 and not first:
                        output(b - 1, DC * NH - 1)
                    if g and g % RUN == 0:
                        output(b, g // RUN - 1)

            V_.memset(ones[:, :], 1.0).then_inc(s_ones, 1)
            step(-1, "ln1")
            split_w1()
            dve.wait_ge(s_b1, 32)
            for s in PRO:
                if s != ("ln1",):
                    step(-1, *s)
                if s == ("q", 0, 1):
                    setup_scales()
            body(0, first=True)
            with dve.Fori(1, NB - 1) as b:
                body(b)
            body(NB - 1, last=True)
            output(NB - 1, DC * NH - 1)
            for s in EPI:
                step(NB, *s)

        @block.tensor
        def _(pe):
            mm = nc.tensor.matmul

            def where(g):
                return g // PHASE, g // RUN % NH, g // T % 2, g % T

            def scores(b, g, first):
                c, h, o, t = where(g)
                if first and g == 0:
                    pe.wait_ge(s_scl, 1)
                if g % PHASE in (0, T // 2):
                    pe.wait_ge(s_stack[c][g % PHASE // (T // 2)], 96 * (b + 1))
                for j in range(4):
                    if j % 2 == 0 and not (first and g == 0):
                        pe.wait_ge(s_silu, 2 * GROUPS * b + 2 * g + j // 2 - 1)
                    head = c * HPC + 2 * j + o
                    ins = mm(SP[:, j, :], KS[:, head, t * P:(t + 1) * P], QS[:, head, h * HALF:(h + 1) * HALF],
                             start=True, stop=True)
                    if j % 2:
                        ins.then_inc(s_score, 1)

            def times_v(b, g, first):
                c, h, o, t = where(g)
                if g % PHASE == 0:
                    pe.wait_ge(s_v, 2 * b + c + 1)
                if g % RUN == 0 and not (first and g < 2 * RUN):
                    pe.wait_ge(s_z, DC * NH * b + g // RUN - 1)
                pe.wait_ge(s_silu, 2 * GROUPS * b + 2 * g + 2)
                for j in range(4):
                    ins = mm(OP[32 * j:32 * j + 32, g // RUN % 2, :], V[:, t, c * HPC // 2 + j, o * DH:o * DH + 2 * DH],
                             attn[:, g % 2, j, :], start=(o == 0 and t == 0), stop=(o == 1 and t == T - 1))
                ins.then_inc(s_av, 1)

            def first_of_bank(b, me):
                return isinstance(b, int) and b == 0 and POS[me] - NPOST < 2

            def step(b, kind, *a):
                me = (kind, *a)
                if me not in POS:
                    return
                k = bank_of(me)
                bank = FP[:, k, :]
                if first_of_bank(b, me):
                    pe.wait_ge(s_setup, 1 + k)
                if not (isinstance(b, int) and turn_of(b, me) <= 1):
                    pe.wait_ge(s_evac[k], turn_of(b, me) - 1)
                if kind in ("xt", "h"):
                    i = a[0]
                    pe.wait_ge(s_norm, (NP + 2 * NP * b + i + 1) if kind == "h" else (2 * NP * (b + 1) + i + 1))
                    for c in range(DC):
                        for j in range(2):
                            ins = nc.tensor.transpose(bank[:, c * PAIR + j * P:c * PAIR + (j + 1) * P],
                                                      normed[:, j, c * P:(c + 1) * P], ident[:, :])
                elif kind in ("k", "q", "u"):
                    c, h = a
                    wait_evacuated(pe, b if is_next(me) else b - 1, ("xt", 2 * h + 1))
                    col = {"u": 0, "q": 2 * D, "k": 3 * D}[kind] + c * P
                    cols = slice(h * HALF, (h + 1) * HALF)
                    passes = [(w, r, kc) for kc in range(DC) for w, r in ((W1h, xh), (W1h, xl), (W1l, xh))]
                    for n, (w, r, kc) in enumerate(passes):
                        ins = mm(bank, w[:, kc, col:col + P], r[:, kc, cols], start=n == 0, stop=n == len(passes) - 1)
                elif kind == "v":
                    i = a[0]
                    wait_evacuated(pe, b, ("xt", i))
                    passes = [(w, r, kc) for kc in range(DC) for w, r in ((W1h, xh), (W1h, xl), (W1l, xh))]
                    for j in range(2):
                        toks = slice((2 * i + j) * P, (2 * i + j + 1) * P)
                        for n, (w, r, kc) in enumerate(passes):
                            ins = mm(bank[:, j * D:(j + 1) * D], r[:, kc, toks], w[:, kc, D:2 * D],
                                     start=n == 0, stop=n == len(passes) - 1)
                elif kind == "f1":
                    t, hf = a
                    pe.wait_ge(s_ht, NP * b + t // 2 + 1)
                    passes = [(r, kc) for kc in range(DC) for r in (hTh, hTl)]
                    for n, (r, kc) in enumerate(passes):
                        ins = mm(bank, r[:, kc, t % 2 * P:(t % 2 + 1) * P], Wq1[:, kc, hf * HALF:(hf + 1) * HALF],
                                 start=n == 0, stop=n == len(passes) - 1)
                elif kind == "g":
                    t, r = a
                    pe.wait_ge(s_hn, NP * b + t // 2 + 1)
                    for n in range(4):
                        col = (4 * r + n) * P
                        ins = nc.tensor.transpose(bank[:, n * P:(n + 1) * P], hid[:, t % 4, col:col + P], ident[:, :])
                elif kind == "f2":
                    t = a[0]
                    passes = [(w, r, n) for r in range(2) for n in range(4) for w in (hgh, hgl)]
                    for i, (w, r, n) in enumerate(passes):
                        if i % 8 == 0:
                            pe.wait_ge(s_hg, 2 * T * b + 2 * t + r + 1)
                        ins = mm(bank[:, 0:D], w[:, r, n * P:(n + 1) * P], Wq2[:, 4 * r + n, :],
                                 start=i == 0, stop=i == len(passes) - 1)
                elif kind == "zt":
                    i = a[0]
                    pe.wait_ge(s_z, DC * NH * b - (i < NP // 2))
                    for j in range(2):
                        for c in range(DC):
                            toks = slice((2 * i + j) * P, (2 * i + j + 1) * P)
                            ins = nc.tensor.transpose(bank[:, j * D + c * P:j * D + (c + 1) * P], uz[:, c, toks], ident[:, :])
                elif kind == "a":
                    i = a[0]
                    for j in range(2):
                        toks = slice((2 * i + j) * P, (2 * i + j + 1) * P)
                        for c in range(DC):
                            ins = mm(bank[:, j * D:(j + 1) * D], uz[:, c, toks], W2c[:, c, :], start=c == 0, stop=c == DC - 1)
                ins.then_inc(s_fill[k], 1)

            def setup_step(g):
                if g == 3:
                    pe.wait_ge(s_bc, 1)
                    wait_evacuated(pe, -1, [s for s in PRO if s[0] in FILLERS and bank_of(s) == 0][-1])
                    for c in range(DC):
                        mm(FP[:, 0, 0:D], onesm[:, :], w2g[:, c * D:(c + 1) * D], start=c == 0, stop=c == DC - 1)
                    for c in range(DC):
                        ins = mm(FP[:, 0, D:2 * D], bcasts[:, c, :], w2raw[:, c * D:(c + 1) * D], start=c == 0, stop=c == DC - 1)
                    ins.then_inc(s_cmm, 1)
                elif g == 5:
                    pe.wait_ge(s_tern, 1)
                    wait_evacuated(pe, -1, [s for s in PRO if s[0] in FILLERS and bank_of(s) == 1][-1])
                    for c in range(HC):
                        ins = mm(FP[:, 1, 0:D], bcasts[:, DC + c, :], Wq2[:, c, :].bitcast(F32), start=c == 0, stop=c == HC - 1)
                    ins.then_inc(s_cmm, 1)

            def body(b, first=False, last=False):
                for g in range(GROUPS):
                    scores(b, g, first)
                    if g == 0 and not first:
                        times_v(b - 1, GROUPS - 1, False)
                    if first:
                        setup_step(g)
                    for s in steps(g, first, last):
                        step(b, *s)
                    if g:
                        times_v(b, g - 1, first)

            pe.wait_ge(s_ident, 1)
            for s in PRO:
                if s == ("k", 0, 0):
                    pe.wait_ge(s_w1s, 1)
                if s == ("v", 0):
                    pe.wait_ge(s_abs, 2)
                    pe.wait_ge(s_ones, 1)
                    mm(SP[:, 0, 0:2], ones[:, :], asum[:, :], start=True, stop=True).then_inc(s_tot, 1)
                step(-1, *s)
            body(0, first=True)
            with pe.Fori(1, NB - 1) as b:
                body(b)
            body(NB - 1, last=True)
            times_v(NB - 1, GROUPS - 1, False)
            for s in EPI:
                step(NB, *s)



def kernel(L0_attn_x, L0_attn_W1, L0_attn_b1, L0_attn_W2, L0_attn_b2, L0_attn_gamma, L0_attn_beta,
           L0_ffn_ln1_g, L0_ffn_ln1_b, L0_ffn_w1, L0_ffn_b1, L0_ffn_ln2_g, L0_ffn_ln2_b, L0_ffn_w2, L0_ffn_b2):
    import numpy as _np
    import concourse.bacc as _bacc
    from concourse import mybir as _mybir
    from concourse.bass_utils import run_bass_kernel_spmd as _run

    def columns(v):
        return _np.ascontiguousarray(_np.asarray(v).reshape(-1, P).T)

    arrays = {
        "x": _np.ascontiguousarray(L0_attn_x),
        "W1": _np.ascontiguousarray(L0_attn_W1),
        "b1": _np.ascontiguousarray(L0_attn_b1),
        "b1c": columns(L0_attn_b1),
        "W2": _np.ascontiguousarray(L0_attn_W2),
        "b2": _np.ascontiguousarray(L0_attn_b2),
        "gamc": columns(L0_attn_gamma),
        "betc": columns(L0_attn_beta),
        "l1gc": columns(L0_ffn_ln1_g),
        "l1bc": columns(L0_ffn_ln1_b),
        "w1T": _np.ascontiguousarray(_np.asarray(L0_ffn_w1).T),
        "fb1": _np.ascontiguousarray(L0_ffn_b1),
        "l2gc": columns(L0_ffn_ln2_g),
        "l2bc": columns(L0_ffn_ln2_b),
        "w2T": _np.ascontiguousarray(_np.asarray(L0_ffn_w2).T),
        "fb2": _np.ascontiguousarray(L0_ffn_b2),
    }
    nc = _bacc.Bacc("TRN2", target_bir_lowering=False, num_devices=1)
    args = [nc.dram_tensor(f"in_{n}", a.shape, _mybir.dt.from_np(a.dtype), kind="ExternalInput").ap()
            for n, a in arrays.items()]
    out = nc.dram_tensor("out_dram", (NB, SEQ, D), _mybir.dt.float32, kind="ExternalOutput").ap()
    hybrid_block_kernel(nc, *args, out)
    r = _run(nc, [{f"in_{n}": a for n, a in arrays.items()}], core_ids=[0])
    return r.results[0]["out_dram"]
```

```python
import numpy as np

import concourse.bass as bass
from concourse import mybir
from contextlib import ExitStack

F32 = mybir.dt.float32
F32R = mybir.dt.float32r
BF16 = mybir.dt.bfloat16
ALU = mybir.AluOpType
ACT = mybir.ActivationFunctionType

P = 128
NB, SEQ, D = 8, 1024, 256
HEADS, DH = 16, 16
HID = 1024
EPS = 1e-5
DC = D // P
HC = HID // P
T = SEQ // P
HPC = P // DH
HALF = 512
NH = SEQ // HALF
PAIR = 2 * P
NP = T // 2
PARTS = 3
QROWS = PARTS * DH
KROWS = (PARTS + 2) * DH
GROUPS = DC * NH * 2 * T
PHASE = GROUPS // DC
RUN = 2 * T
ROUND = 1.5 * 2.0 ** 23

TABLE = (
    "zs.0 zt.0 zs.1 zt.1",
    "a.0 zs.2",
    "a.1",
    "zt.2",
    "zs.3 zt.3",
    "a.2",
    "vs.1 a.3 u.1.0 k.1.0 y.0",
    "q.1.0",
    "u.1.1",
    "k.1.1",
    "u.0.1 px q.1.1 u.0.0 y.2",
    "f1.0.0",
    "f1.0.1",
    "y.1",
    "",
    "f1.1.0 f1.1.1 y.3 gelu.0",
    "f1.2.0 f1.2.1",
    "ln2.0",
    "nrm2.0",
    "f1.3.0 g.0.0",
    "g.0.1",
    "f1.3.1 f2.0",
    "g.1.0",
    "g.1.1 gelu.1 f1.4.0 f1.4.1",
    "ln2.1 f2.1 f1.5.0",
    "nrm2.1 f1.5.1",
    "g.2.0",
    "g.2.1",
    "f2.2",
    "g.3.0",
    "",
    "",
    "g.3.1 f1.6.0 gelu.2",
    "f2.3 f1.6.1 f1.7.0",
    "ln2.2 f1.7.1",
    "",
    "",
    "nrm2.2 ln1",
    "",
    "g.4.0",
    "g.4.1 xn.0",
    "f2.4 g.5.0 g.5.1 gelu.3 xt.0",
    "f2.5 xn.1",
    "xt.1",
    "ln2.3",
    "nrm2.3",
    "k.0.0",
    "g.6.0 xn.2",
    "g.6.1",
    "q.0.0",
    "f2.6",
    "g.7.0",
    "g.7.1",
    "xt.2",
    "xn.3 v.0",
    "v.1 xt.3",
    "",
    "",
    "",
    "f2.7",
    "k.0.1",
    "q.0.1",
    "v.2",
    "v.3 vs.0",
)
SLOTS = [[(n.split(".")[0], *map(int, n.split(".")[1:])) for n in row.split()] for row in TABLE]
assert len(SLOTS) == GROUPS

POST = ("zt", "zs", "a")


def is_next(s):
    return s[0] in ("ln1", "xn", "xt", "v") or s[0] in ("k", "q") and s[1] == 0


FILLERS = ("zt", "a", "u", "f1", "g", "f2", "xt", "k", "q", "v")
ORDER = [s for g in range(GROUPS) for s in SLOTS[g]]
PIECES = [s for s in ORDER if s[0] in FILLERS]
POS = {s: n for n, s in enumerate(PIECES)}
NPOST = sum(s[0] in POST for s in PIECES)
assert all(POS[s] < NPOST for s in PIECES if s[0] in POST) and NPOST % 2 == 0


def in_order(*steps):
    places = [ORDER.index((n.split(".")[0], *map(int, n.split(".")[1:]))) for n in steps]
    assert places == sorted(places), steps


in_order("a.0", "zs.2")
in_order("a.1", "zs.3")
in_order("a.3", "y.0", "f1.1.1", "y.3")
in_order("a.3", "px", "y.1", "ln1")
in_order("px", "y.2", "f1.5.1", "ln1", "xn.0")
in_order("px", "f2.0")
for _n in ("k.1.0", "q.1.0", "k.1.1", "q.1.1", "u.0.0", "u.0.1", "u.1.0", "u.1.1"):
    in_order("a.3", _n, "f1.0.0")
for _i in range(NP):
    in_order(f"y.{_i}", f"f1.{_i}.0")
    in_order(f"nrm2.{_i}", f"g.{2 * _i}.0", f"g.{2 * _i}.1", f"f2.{2 * _i}",
             f"g.{2 * _i + 1}.0", f"g.{2 * _i + 1}.1", f"f2.{2 * _i + 1}")
for _i in range(NP - 2):
    in_order(f"g.{2 * _i + 1}.1", f"f1.{2 * _i + 4}.0")
in_order("g.5.1", "xt.0")
in_order("g.7.1", "xt.2")
assert not {("zs", 2), ("zs", 3)} & set(SLOTS[0])
Y_ORDER = [s[1] for s in ORDER if s[0] == "y"]


def bank_of(step):
    return POS[step] % 2


def pieces_of(bank, kept=lambda s: True, upto=None):
    last = len(PIECES) if upto is None else POS[upto] + 1
    return sum(kept(s) for s in PIECES[:last] if bank_of(s) == bank)


def turn_of(body, step):
    k = bank_of(step)
    if isinstance(body, int) and body < 0:
        return pieces_of(k, is_next, step)
    base = body * pieces_of(k) + pieces_of(k, is_next) - pieces_of(k, lambda s: s[0] in POST)
    if isinstance(body, int) and body == NB:
        base = base - pieces_of(k, is_next)
    if isinstance(body, int) and body == NB - 1:
        return base + pieces_of(k, lambda s: not is_next(s), step)
    return base + pieces_of(k, upto=step)


def hybrid_block_kernel(nc, x, W1, b1, b1c, W2, b2, gamc, betc, l1gc, l1bc, w1T, fb1, l2gc, l2bc, w2T, fb2, out):
    xv = x.rearrange("b (p t) d -> b p t d", p=P)
    ov = out.rearrange("b (p t) d -> b p t d", p=P)
    kd = [nc.dram_tensor(f"k_scratch{c}", [HPC, KROWS, SEQ], BF16, kind="Internal").ap() for c in range(DC)]
    qd = [nc.dram_tensor(f"q_scratch{c}", [HPC, QROWS, SEQ], BF16, kind="Internal").ap() for c in range(DC)]

    ctx = ExitStack()
    with ctx:
        top = [nc.sbuf_base + (-nc.sbuf_base) % 64]

        def at(name, shape, dt, offset):
            return nc.alloc_sbuf_tensor_at(name, shape, dt, offset=offset)

        def sb(name, shape, dt):
            offset = top[0]
            size = int(np.prod(shape[1:])) * (2 if dt == BF16 else 4)
            top[0] = offset + size + (-size) % 32
            return at(name, shape, dt, offset)

        qs_at = top[0]
        QS = sb("QS", [P, HEADS, SEQ], BF16)
        KS = sb("KS", [P, HEADS, SEQ], BF16)
        V = sb("V", [P, T, HEADS // 2, 3 * DH], F32)
        uz_at = top[0]
        uz = sb("uz", [P, DC, SEQ], F32)
        attn_at = top[0]
        attn = sb("attn", [P, 2, 4, HALF], F32)
        W1h = sb("W1h", [P, DC, 4 * D], F32R)
        W1l = sb("W1l", [P, DC, 4 * D], F32R)
        Wq1 = sb("Wq1", [P, DC, HID], F32R)
        Wq2 = sb("Wq2", [P, HC, D], F32R)
        W2h = sb("W2h", [P, DC, D], F32R)
        W2l = sb("W2l", [P, DC, D], F32R)
        vraw = sb("vraw", [P, T, D], F32)
        xh_at = top[0]
        xp = sb("xp", [P, NP, 2, DC, PAIR], F32R)
        hid = at("hid", [P, 4, HID], F32, xh_at)
        hT_at = top[0]
        yT = sb("yT", [P, 2, DC, PAIR], F32R)
        hg_at = top[0]
        hgh = sb("hgh", [P, 2, HALF], F32R)
        hgl = sb("hgl", [P, 2, HALF], F32R)
        part_at = top[0]
        part = sb("part", [P, T, D], F32)
        xin_at = top[0]
        xin = sb("xin", [P, T, D], F32)
        yX = at("yX", [P, NP - 2, 2, DC, PAIR], F32R, xin_at)
        fb1b = sb("fb1b", [P, HID], F32)
        kst = sb("kst", [P, PARTS, HALF], BF16)
        qst = sb("qst", [P, PARTS, HALF], BF16)
        qkf = sb("qkf", [P, HALF], F32)
        normed = sb("normed", [P, 2, D], F32)
        tmp = sb("tmp", [P, HALF], F32)
        bvb = sb("bvb", [P, D], F32)
        cst = sb("cst", [P, D], F32)
        ident = sb("ident", [P, P], F32)
        b1s = sb("b1s", [P, 4 * DC], F32)
        gam = sb("gam", [P, DC], F32)
        bet = sb("bet", [P, DC], F32)
        l1g = sb("l1g", [P, DC], F32)
        l1b = sb("l1b", [P, DC], F32)
        l2g = sb("l2g", [P, HC], F32)
        l2b = sb("l2b", [P, HC], F32)
        epst = sb("epst", [P, 2 * T], F32)
        mhalf = sb("mhalf", [P, 2 * T], F32)
        st1 = sb("st1", [P, T, 6], F32)
        mv1 = sb("mv1", [P, T, 2], F32)
        rp1 = sb("rp1", [P, 2 * T], F32)
        rs1 = sb("rs1", [P, 2 * T], F32)
        rat = sb("rat", [P, T], F32)
        ratq = sb("ratq", [P, T], F32)
        st2 = sb("st2", [P, 2, 2, 6], F32)
        mv2 = sb("mv2", [P, 2, 2], F32)
        rp2 = sb("rp2", [P, 2], F32)
        rs2 = sb("rs2", [P, 2], F32)
        st3 = sb("st3", [P, 2, 6], F32)
        mv3 = sb("mv3", [P, T, 2], F32)
        rp3 = sb("rp3", [P, 2], F32)
        rs3 = sb("rs3", [P, T], F32)
        asum = sb("asum", [P, 2], F32)
        cm = sb("cm", [P, 2], F32)
        scl = sb("scl", [P, 2], F32)
        cq = sb("cq", [P, 2], F32)
        zX = at("zX", [P, 2, DC, PAIR], F32R, hg_at)
        w1raw = at("w1raw", [P, DC, 4 * D], F32, attn_at)
        wfraw = at("wfraw", [P, DC, HID], F32, qs_at + 2 * HPC * SEQ)
        wsraw = at("wsraw", [P, HC, D], F32, qs_at + 2 * HPC * SEQ + 4 * DC * HID)
        w2raw = at("w2raw", [P, DC * D], F32, hT_at)
        b2b = at("b2b", [P, D], F32, hT_at + 4 * DC * D)
        fb2b = at("fb2b", [P, D], F32, hT_at + 4 * (DC + 1) * D)
        bcasts = at("bcasts", [P, 2 * DC + HC, P], F32, uz_at)
        ones = at("ones", [P, P], F32, uz_at + 4 * (2 * DC + HC) * P)
        onesm = at("onesm", [P, P], F32, uz_at + 4 * (2 * DC + HC + 1) * P)
        junk = at("junk", [P, HC * D], F32, part_at)
        w2g = tmp

        SP = ctx.enter_context(nc.psum_tensor("scores", [P, 4, HALF], F32))
        OP = ctx.enter_context(nc.psum_tensor("outs", [P, 2, HALF], F32))
        FP = ctx.enter_context(nc.psum_tensor("fill", [P, 2, HALF], F32))

        def sem(name):
            return ctx.enter_context(nc.semaphore(name))

        s_w1 = sem("w1_loaded")
        s_w1s = sem("w1_split")
        s_b1 = sem("projection_biases_loaded")
        s_wf = sem("wf_loaded")
        s_ws = sem("ws_loaded")
        s_vec = sem("vectors_loaded")
        s_abs = sem("abs_summed")
        s_tot = sem("abs_total")
        s_ident = sem("identity_made")
        s_const = sem("pool_constants")
        s_ones = sem("ones_made")
        s_bc = sem("setup_operands")
        s_tern = sem("ternary_weights")
        s_cmm = sem("setup_products")
        s_setup = sem("setup_done")
        s_x = sem("x_loaded")
        s_norm = sem("normed_pair")
        s_mv1, s_rs1 = sem("input_moments"), sem("input_rstd")
        s_rat = sem("ratio_of_rstds")
        s_mv2, s_rs2 = sem("hidden_moments"), sem("hidden_rstd")
        s_mv3, s_rs3 = sem("z_moments"), sem("z_rstd")
        s_fill = [sem("filled0"), sem("filled1")]
        s_evac = [sem("evacuated0"), sem("evacuated1")]
        s_xh = sem("x_high_part")
        s_split = sem("qk_split")
        s_kw = sem("k_parts_written")
        s_qw = sem("q_parts_written")
        s_stack = [[sem(f"stacked{c}_{h}") for h in range(NH)] for c in range(DC)]
        s_v = sem("v_ready")
        s_score = sem("scores_ready")
        s_silu = sem("attn_ready")
        s_av = sem("av_done")
        s_z = sem("z_ready")
        s_zs = sem("z_split")
        s_ht = sem("h_split")
        s_gelu = sem("gelu_done")
        s_hn = sem("hidden_normed")
        s_hg = sem("hidden_split")
        s_out = sem("out_written")

        block = ctx.enter_context(nc.Block())

        def wait_filled(eng, b, step):
            eng.wait_ge(s_fill[bank_of(step)], turn_of(b, step))

        def wait_evacuated(eng, b, step):
            eng.wait_ge(s_evac[bank_of(step)], turn_of(b, step))

        def y_of(i):
            return yT if i in (0, NP - 1) else yX[:, i - 1, :, :, :]

        def z_of(i):
            return zX if i % 2 else yT

        def hid_of(t):
            return hid[:, t % 4, :]

        def steps(g, first, last):
            for s in SLOTS[g]:
                if first and s[0] in POST or last and (is_next(s) or s == ("vs", 0)):
                    continue
                yield s

        PRO = [s for s in ORDER if is_next(s) or s == ("vs", 0)]
        EPI = [s for s in ORDER if s[0] in POST]

        def last_filler(bank):
            return [s for s in PRO if s in POS and bank_of(s) == bank][-1]

        @block.sync
        def _(sp):
            def load_x(b):
                sp.dma_start(xin[:, :, :], xv[b, :, :, :]).then_inc(s_x, 16)

            def write_parts(b, c, h):
                if c == 0 and h == 0:
                    for cc in range(DC):
                        for hh in range(NH):
                            sp.wait_ge(s_stack[cc][hh], 96 * b)
                cols = slice(h * HALF, (h + 1) * HALF)
                n = 2 * (NH * c + h)
                sp.wait_ge(s_split, 8 * b + n + 1)
                for r in range(PARTS + 2):
                    sp.dma_start(kd[c][:, r * DH:(r + 1) * DH, cols], kst[:, r % PARTS, :]).then_inc(s_kw, 16)
                sp.wait_ge(s_split, 8 * b + n + 2)
                for r in range(PARTS):
                    sp.dma_start(qd[c][:, r * DH:(r + 1) * DH, cols], qst[:, r, :]).then_inc(s_qw, 16)

            def load_stack(b, c, h, reused):
                sp.wait_ge(s_kw, 320 * b + 80 * (NH * c + h + 1))
                sp.wait_ge(s_qw, 48 * (4 * b + NH * c + h + 1))
                if reused:
                    sp.wait_ge(s_score, 2 * GROUPS * (b - 1) + 2 * PHASE * (c + 1))
                heads = slice(c * HPC, (c + 1) * HPC)
                cols = slice(h * HALF, (h + 1) * HALF)
                for i, first in enumerate((1, 2, 0)):
                    rows = QROWS if i < 2 else P - 2 * QROWS
                    dst = slice(i * QROWS, i * QROWS + rows)
                    sp.dma_start(KS[dst, heads, cols],
                                 kd[c][:, first * DH:first * DH + rows, cols].rearrange("h r n -> r h n")).then_inc(s_stack[c][h], 16)
                    sp.dma_start(QS[dst, heads, cols],
                                 qd[c][:, 0:rows, cols].rearrange("h r n -> r h n")).then_inc(s_stack[c][h], 16)

            def store(b):
                for i in range(2):
                    wait_evacuated(sp, b + 1, ("a", 2 * i + 1))
                    ts = slice(i * T // 2, (i + 1) * T // 2)
                    sp.dma_start(ov[b, :, ts, :], part[:, ts, :]).then_inc(s_out, 16)

            def body(b, first=False, last=False):
                if not first:
                    store(b - 1)
                for h in range(NH):
                    write_parts(b, 1, h)
                    if first and h == 0:
                        sp.wait_ge(s_tern, 2)
                    load_stack(b, 1, h, not first)
                if not last:
                    wait_evacuated(sp, b, ("f1", T - 3, 1))
                    load_x(b + 1)
                    for h in range(NH):
                        write_parts(b + 1, 0, h)
                        load_stack(b + 1, 0, h, True)

            load_x(0)
            sp.dma_start(w1raw[:, :, :], W1.rearrange("(c p) n -> p c n", p=P)).then_inc(s_w1, 16)
            sp.dma_start(b1s[:, :], b1c).then_inc(s_b1, 16)
            sp.dma_start(bvb[:, :], b1[D:2 * D].partition_broadcast(P)).then_inc(s_b1, 16)
            sp.dma_start(wfraw[:, :, :], w1T.rearrange("(c p) n -> p c n", p=P)).then_inc(s_wf, 16)
            sp.dma_start(wsraw[:, :, :], w2T.rearrange("(c p) n -> p c n", p=P)).then_inc(s_ws, 16)
            sp.dma_start(w2raw[:, :].rearrange("p (c n) -> p c n", c=DC), W2.rearrange("(c p) n -> p c n", p=P)).then_inc(s_vec, 16)
            for dst, src in ((gam, gamc), (bet, betc), (l1g, l1gc), (l1b, l1bc), (l2g, l2gc), (l2b, l2bc)):
                sp.dma_start(dst[:, :], src).then_inc(s_vec, 16)
            for dst, src in ((fb1b, fb1), (b2b, b2), (fb2b, fb2)):
                sp.dma_start(dst[:, :], src.partition_broadcast(P)).then_inc(s_vec, 16)
            for h in range(NH):
                write_parts(0, 0, h)
                load_stack(0, 0, h, False)
            body(0, first=True)
            with sp.Fori(1, NB - 1) as b:
                body(b)
            body(NB - 1, last=True)
            store(NB - 1)
            sp.wait_ge(s_out, 32 * NB)

        @block.gpsimd
        def _(pool):
            nc.gpsimd.memset(ident[:, :], 0.0)
            nc.gpsimd.memset(epst[:, :], EPS).then_inc(s_const, 1)
            nc.gpsimd.memset(mhalf[:, :], -0.5).then_inc(s_const, 1)
            pool.drain()
            nc.gpsimd.affine_select(out=ident[:, :], in_=ident[:, :], compare_op=ALU.not_equal, fill=1.0,
                                    base=0, pattern=[[-1, P]], channel_multiplier=1).then_inc(s_ident, 1)

            def rsqrt(out_ap, in_ap, tmp_ap, n, done):
                nc.gpsimd.tensor_tensor(tmp_ap, in_ap, epst[:, 0:n], ALU.add)
                pool.drain()
                nc.gpsimd.tensor_tensor(out_ap, tmp_ap, mhalf[:, 0:n], ALU.pow).then_inc(done, 1)

            def input_rstd(b):
                pool.wait_ge(s_mv1, b + 1)
                nc.gpsimd.tensor_tensor(rp1[:, 0:T], mv1[:, :, 1], epst[:, 0:T], ALU.add)
                pool.drain()
                nc.gpsimd.tensor_tensor(rs1[:, 0:T], rp1[:, 0:T], mhalf[:, 0:T], ALU.pow).then_inc(s_rs1, 1)
                nc.gpsimd.tensor_tensor(rp1[:, T:2 * T], rp1[:, 0:T], epst[:, 0:T], ALU.mult)
                pool.drain()
                nc.gpsimd.tensor_tensor(rp1[:, T:2 * T], rp1[:, T:2 * T], mv1[:, :, 1], ALU.add)
                pool.drain()
                nc.gpsimd.tensor_tensor(rs1[:, T:2 * T], rp1[:, T:2 * T], mhalf[:, T:2 * T], ALU.pow)
                pool.drain()
                nc.gpsimd.tensor_tensor(rat[:, :], rs1[:, 0:T], rs1[:, T:2 * T], ALU.mult)
                pool.drain()
                nc.gpsimd.tensor_tensor(rat[:, :], rat[:, :], rp1[:, 0:T], ALU.mult).then_inc(s_rat, 1)

            def step(b, kind, *a):
                if kind in ("zt", "ln2", "ln1"):
                    pool.drain()
                if kind == "zt":
                    pool.wait_ge(s_mv3, NP * (b - 1) + a[0] + 1)
                    rsqrt(rs3[:, 2 * a[0]:2 * a[0] + 2], mv3[:, 2 * a[0]:2 * a[0] + 2, 1], rp3[:, :], 2, s_rs3)
                elif kind == "ln2":
                    pool.wait_ge(s_mv2, NP * b + a[0] + 1)
                    rsqrt(rs2[:, :], mv2[:, :, 1], rp2[:, :], 2, s_rs2)
                elif kind == "ln1":
                    input_rstd(b + 1)

            def body(b, first=False, last=False):
                for g in range(GROUPS):
                    for s in steps(g, first, last):
                        step(b, *s)

            pool.wait_ge(s_const, 2)
            step(-1, "ln1")
            nc.gpsimd.memset(V[:, :, :, :], 0.0).then_inc(s_const, 1)
            body(0, first=True)
            with pool.Fori(1, NB - 1) as b:
                body(b)
            body(NB - 1, last=True)
            for s in EPI:
                step(NB, *s)

        @block.scalar
        def _(act):
            def silu_group(b, g, first):
                for hf in range(2):
                    act.wait_ge(s_score, 2 * GROUPS * b + 2 * g + hf + 1)
                    nc.scalar.activation(attn[:, g % 2, 2 * hf:2 * hf + 2, :], SP[:, 2 * hf:2 * hf + 2, :],
                                         ACT.Silu).then_inc(s_silu, 1)

            def project(b, step, out_ap, col):
                wait_filled(act, b, step)
                k = bank_of(step)
                nc.scalar.activation(out_ap, FP[:, k, :], ACT.Silu, bias=b1s[:, col:col + 1]).then_inc(s_evac[k], 1)

            def place_v(b, c, reused):
                wait_evacuated(act, b - 1, ("v", NP - 1))
                if reused:
                    act.wait_ge(s_av, GROUPS * (b - 1) + PHASE * (c + 1))
                pairs = slice(c * HPC // 2, (c + 1) * HPC // 2)
                src = vraw[:, :, c * P:(c + 1) * P].rearrange("p t (j o d) -> p t j o d", o=2, d=DH)
                for o in range(2):
                    ins = nc.scalar.activation(V[:, :, pairs, 2 * o * DH:2 * o * DH + DH], src[:, :, :, o, :], ACT.Silu)
                ins.then_inc(s_v, 1)

            def step(b, first, kind, *a):
                me = (kind, *a)
                if kind == "xt":
                    wait_filled(act, b, me)
                    k, i = bank_of(me), a[0]
                    nc.scalar.activation(xp[:, i, 0, :, :],
                                         FP[:, k, :].rearrange("p (c n) -> p c n", c=DC), ACT.Copy).then_inc(s_xh, 1)
                elif kind in ("k", "q"):
                    c, h = a
                    n = 2 * (NH * c + h) + (kind == "q")
                    act.wait_ge(s_split, 8 * (b + 1 - c) + n)
                    project(b, me, qkf[:, :], (3 if kind == "k" else 2) * DC + c)
                elif kind == "u":
                    c, h = a
                    project(b, me, uz[:, c, h * HALF:(h + 1) * HALF], c)
                elif kind == "vs":
                    place_v(b if a[0] else b + 1, a[0], not (first and a[0] == 1))
                elif kind == "gelu":
                    i = a[0]
                    wait_evacuated(act, b, ("f1", 2 * i + 1, 1))
                    rows = hid[:, 2 * i % 4:2 * i % 4 + 2, :]
                    nc.scalar.activation(rows, rows, ACT.Gelu).then_inc(s_gelu, 1)

            def body(b, first=False, last=False):
                for g in range(GROUPS):
                    silu_group(b, g, first)
                    for s in steps(g, first, last):
                        step(b, first, *s)

            def sum_of_abs(i):
                w, loaded = ((wfraw, s_wf), (wsraw, s_ws))[i]
                act.wait_ge(loaded, 16)
                if i:
                    act.wait_ge(s_abs, i)
                nc.scalar.activation(junk[:, :], w[:, :, :].rearrange("p c n -> p (c n)"), ACT.Abs,
                                     accum_out=asum[:, i:i + 1]).then_inc(s_abs, 1)

            nc.scalar.preload_act_table(ACT.Silu)
            act.wait_ge(s_b1, 32)
            for s in PRO:
                if s[0] == "vs":
                    act.wait_ge(s_const, 3)
                    place_v(0, 0, False)
                else:
                    step(-1, True, *s)
                if s[0] == "q":
                    sum_of_abs(s[2])
            body(0, first=True)
            with act.Fori(1, NB - 1) as b:
                body(b)
            body(NB - 1, last=True)

        @block.vector
        def _(dve):
            V_ = nc.vector

            def split_w1(rest):
                if not rest:
                    dve.wait_ge(s_w1, 16)
                    V_.tensor_copy(W1h[:, :, :], w1raw[:, :, :])
                else:
                    V_.tensor_tensor(W1l[:, :, :], w1raw[:, :, :], W1h[:, :, :].bitcast(F32),
                                     ALU.subtract).then_inc(s_w1s, 1)

            def setup_broadcasts():
                V_.memset(onesm[:, :], 1.0 / D)
                dve.wait_ge(s_vec, 16 * 10)
                for c in range(DC):
                    cols = slice(c * D, (c + 1) * D)
                    V_.tensor_scalar(w2g[:, cols], w2raw[:, cols], gam[:, c:c + 1], None, ALU.mult)
                dve.wait_ge(s_ones, 1)
                for n in range(2 * DC + HC):
                    v = (bet[:, n:n + 1] if n < DC else l2b[:, n - DC:n - DC + 1] if n < DC + HC
                         else l1b[:, n - DC - HC:n - DC - HC + 1])
                    ins = V_.tensor_scalar(bcasts[:, n, :], ones[:, :], v, None, ALU.mult)
                ins.then_inc(s_bc, 1)

            def setup_scales():
                dve.wait_ge(s_tot, 1)
                V_.tensor_scalar(cm[:, :], OP[:, 1, 0:2], 1.0 / (D * HID), 1e-5, ALU.mult, ALU.max)
                dve.drain()
                V_.reciprocal(scl[:, :], cm[:, :])
                dve.drain()
                V_.reciprocal(cq[:, :], scl[:, :])

            def setup_ternary(raw, q, scale):
                dve.drain()
                V_.tensor_scalar(raw[:, :, :], raw[:, :, :], scale, 1.0, ALU.mult, ALU.min)
                dve.drain()
                V_.tensor_scalar(raw[:, :, :], raw[:, :, :], -1.0, ROUND, ALU.max, ALU.add)
                dve.drain()
                V_.tensor_scalar(q[:, :, :], raw[:, :, :], ROUND, None, ALU.subtract).then_inc(s_tern, 1)

            def setup_w2():
                dve.wait_ge(s_cmm, 1)
                for c in range(DC):
                    cols = slice(c * D, (c + 1) * D)
                    V_.tensor_tensor(w2g[:, cols], w2g[:, cols], FP[:, 0, 0:D], ALU.subtract)
                V_.tensor_tensor(cst[:, :], FP[:, 0, D:2 * D], b2b[:, :], ALU.add).then_inc(s_setup, 1)
                dve.drain()
                centred = w2g[:, :].rearrange("p (c n) -> p c n", c=DC)
                V_.tensor_copy(W2h[:, :, :], centred)
                dve.drain()
                V_.tensor_tensor(W2l[:, :, :], centred, W2h[:, :, :].bitcast(F32), ALU.subtract)

            def setup_hidden():
                dve.drain()
                dve.wait_ge(s_cmm, 2)
                V_.scalar_tensor_tensor(out=junk[:, 0:D], in0=FP[:, 1, 0:D], scalar=cq[:, 1:2], in1=fb2b[:, :],
                                        op0=ALU.mult, op1=ALU.add).then_inc(s_setup, 1)
                dve.drain()
                V_.tensor_tensor(cst[:, :], cst[:, :], junk[:, 0:D], ALU.add)

            def setup_input():
                for h in range(2):
                    cols = slice(h * HALF, (h + 1) * HALF)
                    dve.wait_ge(s_cmm, 3 + h)
                    V_.scalar_tensor_tensor(out=fb1b[:, cols], in0=FP[:, h, :], scalar=cq[:, 0:1], in1=fb1b[:, cols],
                                            op0=ALU.mult, op1=ALU.add).then_inc(s_setup, 1)

            def stats(rows, st, mv, done):
                for j, views in enumerate(rows):
                    for n, v in enumerate(views):
                        V_.bn_stats(st[:, j, n, :] if len(views) > 1 else st[:, j, :], v)
                dve.drain()
                for j, views in enumerate(rows):
                    src = st[:, j, :, :].rearrange("p a b -> p (a b)") if len(views) > 1 else st[:, j, :]
                    ins = V_.bn_aggr(mv[:, j, :], src)
                ins.then_inc(done, 1)

            def norm_pair(i, after):
                if after is not None:
                    wait_filled(dve, *after)
                for j in range(2):
                    t = 2 * i + j
                    ins = V_.tensor_scalar(normed[:, j, :], xin[:, t, :], mv1[:, t, 0:1], rs1[:, t:t + 1],
                                           ALU.subtract, ALU.mult)
                ins.then_inc(s_norm, 1)

            def output(b, o):
                c, h = o // NH, o % NH
                dve.wait_ge(s_av, GROUPS * b + RUN * (o + 1))
                wait_evacuated(dve, b, ("u", c, h))
                z = uz[:, c, h * HALF:(h + 1) * HALF]
                V_.scalar_tensor_tensor(out=z, in0=OP[:, o % 2, :], scalar=1.0 / SEQ, in1=z,
                                        op0=ALU.mult, op1=ALU.mult).then_inc(s_z, 1)

            def step(b, kind, *a):
                dve.drain()
                me = (kind, *a)
                k = bank_of(me) if me in POS else None
                if kind == "zt":
                    i = a[0]
                    wait_filled(dve, b, me)
                    for j in range(2):
                        ins = V_.bn_stats(st3[:, j, :], FP[:, k, j * D:(j + 1) * D])
                    ins.then_inc(s_evac[k], 1)
                    dve.drain()
                    for j in range(2):
                        ins = V_.bn_aggr(mv3[:, 2 * i + j, :], st3[:, j, :])
                    ins.then_inc(s_mv3, 1)
                elif kind == "zs":
                    i = a[0]
                    z = uz[:, :, i * PAIR:(i + 1) * PAIR]
                    V_.tensor_copy(z_of(i)[:, 0, :, :], z)
                    dve.drain()
                    V_.tensor_tensor(z_of(i)[:, 1, :, :], z, z_of(i)[:, 0, :, :].bitcast(F32), ALU.subtract).then_inc(s_zs, 1)
                elif kind == "a":
                    i = a[0]
                    wait_filled(dve, b, me)
                    dve.wait_ge(s_rs3, NP * (b - 1) + i + 1)
                    for j in range(2):
                        t = 2 * i + j
                        ins = V_.scalar_tensor_tensor(out=part[:, t, :], in0=FP[:, k, j * D:(j + 1) * D],
                                                      scalar=rs3[:, t:t + 1], in1=part[:, t, :],
                                                      op0=ALU.mult, op1=ALU.add)
                    ins.then_inc(s_evac[k], 1)
                elif kind == "px":
                    dve.wait_ge(s_out, 32 * b)
                    V_.tensor_tensor(part[:, :, :], xin[:, :, :],
                                     cst[:, :].unsqueeze(1).broadcast_to([P, T, D]), ALU.add)
                elif kind == "y":
                    i = a[0]
                    if i == 0:
                        dve.wait_ge(s_rat, b + 1)
                        V_.tensor_scalar(ratq[:, :], rat[:, :], cq[:, 0:1], None, ALU.mult)
                    y = tmp[:, :].rearrange("p (c n) -> p c n", c=DC)
                    V_.tensor_tensor(y, xp[:, i, 0, :, :].bitcast(F32), xp[:, i, 1, :, :].bitcast(F32), ALU.add)
                    dve.drain()
                    for c in range(DC):
                        V_.tensor_scalar(y[:, c, :], y[:, c, :], l1g[:, c:c + 1], None, ALU.mult)
                    dve.drain()
                    V_.tensor_copy(y_of(i)[:, 0, :, :], y)
                    dve.drain()
                    V_.tensor_tensor(y_of(i)[:, 1, :, :], y, y_of(i)[:, 0, :, :].bitcast(F32),
                                     ALU.subtract).then_inc(s_ht, 1)
                elif kind == "f1":
                    t, hf = a
                    wait_filled(dve, b, me)
                    cols = slice(hf * HALF, (hf + 1) * HALF)
                    V_.scalar_tensor_tensor(out=hid_of(t)[:, cols], in0=FP[:, k, :], scalar=ratq[:, t:t + 1],
                                            in1=fb1b[:, cols], op0=ALU.mult, op1=ALU.add).then_inc(s_evac[k], 1)
                elif kind == "ln2":
                    i = a[0]
                    dve.wait_ge(s_gelu, NP * b + i + 1)
                    stats([[hid_of(2 * i + j)[:, n * HALF:(n + 1) * HALF] for n in range(2)] for j in range(2)],
                          st2, mv2, s_mv2)
                elif kind == "nrm2":
                    i = a[0]
                    dve.wait_ge(s_rs2, NP * b + i + 1)
                    for j in range(2):
                        row = hid_of(2 * i + j)
                        ins = V_.tensor_scalar(row, row, mv2[:, j, 0:1], rs2[:, j:j + 1], ALU.subtract, ALU.mult)
                    ins.then_inc(s_hn, 1)
                elif kind == "g":
                    t, r = a
                    wait_filled(dve, b, me)
                    V_.tensor_tensor(tmp[:, :].rearrange("p (c n) -> p c n", n=P),
                                     FP[:, k, :].rearrange("p (c n) -> p c n", n=P),
                                     l2g[:, 4 * r:4 * r + 4].unsqueeze(2).broadcast_to([P, 4, P]),
                                     ALU.mult).then_inc(s_evac[k], 1)
                    dve.drain()
                    V_.tensor_copy(hgh[:, r, :], tmp[:, :])
                    dve.drain()
                    V_.tensor_tensor(hgl[:, r, :], tmp[:, :], hgh[:, r, :].bitcast(F32), ALU.subtract).then_inc(s_hg, 1)
                elif kind == "f2":
                    t = a[0]
                    wait_filled(dve, b, me)
                    V_.scalar_tensor_tensor(out=part[:, t, :], in0=FP[:, k, 0:D], scalar=cq[:, 1:2],
                                            in1=part[:, t, :], op0=ALU.mult, op1=ALU.add).then_inc(s_evac[k], 1)
                elif kind == "ln1":
                    dve.wait_ge(s_x, 16 * (b + 2))
                    stats([[xin[:, t, :]] for t in range(T)], st1, mv1, s_mv1)
                elif kind == "xn":
                    i = a[0]
                    if i == 0:
                        dve.wait_ge(s_rs1, b + 2)
                    norm_pair(i, (b, ("xt", i - 1)) if i else None)
                elif kind == "xt":
                    i = a[0]
                    dve.wait_ge(s_xh, NP * (b + 1) + i + 1)
                    V_.tensor_tensor(xp[:, i, 1, :, :], FP[:, k, :].rearrange("p (c n) -> p c n", c=DC),
                                     xp[:, i, 0, :, :].bitcast(F32), ALU.subtract).then_inc(s_evac[k], 1)
                elif kind in ("k", "q"):
                    c, h = a
                    dst, wrote, each = (kst, s_kw, 80) if kind == "k" else (qst, s_qw, 48)
                    wait_evacuated(dve, b, me)
                    dve.wait_ge(wrote, each * (4 * (b + 1 - c) + NH * c + h))
                    V_.tensor_copy(dst[:, 0, :], qkf[:, :])
                    dve.drain()
                    V_.tensor_tensor(qkf[:, :], qkf[:, :], dst[:, 0, :], ALU.subtract)
                    dve.drain()
                    V_.tensor_copy(dst[:, 1, :], qkf[:, :])
                    dve.drain()
                    V_.tensor_tensor(dst[:, 2, :], qkf[:, :], dst[:, 1, :], ALU.subtract).then_inc(s_split, 1)
                elif kind == "v":
                    i = a[0]
                    wait_filled(dve, b, me)
                    if i == 0:
                        dve.wait_ge(s_v, 2 * (b + 1))
                    V_.tensor_tensor(vraw[:, 2 * i:2 * i + 2, :], FP[:, k, :].rearrange("p (t n) -> p t n", t=2),
                                     bvb[:, :].unsqueeze(1).broadcast_to([P, 2, D]), ALU.add).then_inc(s_evac[k], 1)

            def setup_step(g):
                if g == 0:
                    dve.drain()
                    setup_scales()
                    setup_broadcasts()
                    setup_ternary(wsraw, Wq2, scl[:, 1:2])
                elif g == 3:
                    setup_w2()
                    setup_ternary(wfraw, Wq1, scl[:, 0:1])
                elif g == 5:
                    setup_hidden()
                    setup_input()

            def body(b, first=False, last=False):
                for g in range(GROUPS):
                    if first:
                        setup_step(g)
                    for s in steps(g, first, last):
                        step(b, *s)
                    if g == 0 and not first:
                        output(b - 1, DC * NH - 1)
                    if g and g % RUN == 0:
                        output(b, g // RUN - 1)

            V_.memset(ones[:, :], 1.0).then_inc(s_ones, 1)
            step(-1, "ln1")
            split_w1(False)
            dve.wait_ge(s_b1, 32)
            for s in PRO:
                if s != ("ln1",):
                    step(-1, *s)
                if s == ("xn", 0):
                    split_w1(True)
            body(0, first=True)
            with dve.Fori(1, NB - 1) as b:
                body(b)
            body(NB - 1, last=True)
            output(NB - 1, DC * NH - 1)
            for s in EPI:
                step(NB, *s)

        @block.tensor
        def _(pe):
            mm = nc.tensor.matmul

            def where(g):
                return g // PHASE, g // RUN % NH, g // T % 2, g % T

            def scores(b, g, first):
                c, h, o, t = where(g)
                if g % PHASE in (0, T // 2):
                    pe.wait_ge(s_stack[c][g % PHASE // (T // 2)], 96 * (b + 1))
                for j in range(4):
                    if j % 2 == 0 and not (first and g == 0):
                        pe.wait_ge(s_silu, 2 * GROUPS * b + 2 * g + j // 2 - 1)
                    head = c * HPC + 2 * j + o
                    ins = mm(SP[:, j, :], KS[:, head, t * P:(t + 1) * P], QS[:, head, h * HALF:(h + 1) * HALF],
                             start=True, stop=True)
                    if j % 2:
                        ins.then_inc(s_score, 1)

            def times_v(b, g, first, last=False):
                c, h, o, t = where(g)
                if g % PHASE == 0:
                    pe.wait_ge(s_v, 2 * b + c + 1)
                if g % RUN == 0 and not (first and g < 2 * RUN):
                    pe.wait_ge(s_z, DC * NH * b + g // RUN - 1)
                if last:
                    pe.wait_ge(s_silu, 2 * GROUPS * b + 2 * g + 2)
                for j in range(4):
                    ins = mm(OP[32 * j:32 * j + 32, g // RUN % 2, :], V[:, t, c * HPC // 2 + j, o * DH:o * DH + 2 * DH],
                             attn[:, g % 2, j, :], start=(o == 0 and t == 0), stop=(o == 1 and t == T - 1))
                ins.then_inc(s_av, 1)

            def first_of_bank(b, me):
                return isinstance(b, int) and b == 0 and POS[me] - NPOST < 2

            def step(b, kind, *a):
                me = (kind, *a)
                if me not in POS:
                    return
                k = bank_of(me)
                bank = FP[:, k, :]
                if first_of_bank(b, me):
                    pe.wait_ge(s_setup, 3 + k)
                if not (isinstance(b, int) and turn_of(b, me) <= 1):
                    pe.wait_ge(s_evac[k], turn_of(b, me) - 1)
                passes = [(w, part, kc) for kc in range(DC) for w, part in ((W1h, 0), (W1h, 1), (W1l, 0))]
                if kind == "xt":
                    i = a[0]
                    pe.wait_ge(s_norm, NP * (b + 1) + i + 1)
                    for c in range(DC):
                        for j in range(2):
                            ins = nc.tensor.transpose(bank[:, c * PAIR + j * P:c * PAIR + (j + 1) * P],
                                                      normed[:, j, c * P:(c + 1) * P], ident[:, :])
                elif kind in ("k", "q", "u"):
                    c, h = a
                    if me == ("k", 0, h):
                        wait_evacuated(pe, b, ("xt", 2 * h + 1))
                    col = {"u": 0, "q": 2 * D, "k": 3 * D}[kind] + c * P
                    for n, (w, part, kc) in enumerate(passes):
                        ins = mm(bank.rearrange("p (i n) -> p i n", i=2), w[:, kc, col:col + P],
                                 xp[:, 2 * h:2 * h + 2, part, kc, :], start=n == 0, stop=n == len(passes) - 1)
                elif kind == "v":
                    i = a[0]
                    if POS[me] < POS[("k", 0, i // 2)]:
                        wait_evacuated(pe, b, ("xt", i))
                    for j in range(2):
                        for n, (w, part, kc) in enumerate(passes):
                            ins = mm(bank[:, j * D:(j + 1) * D], xp[:, i, part, kc, j * P:(j + 1) * P],
                                     w[:, kc, D:2 * D], start=n == 0, stop=n == len(passes) - 1)
                elif kind == "f1":
                    t, hf = a
                    if t % 2 == 0 and hf == 0:
                        pe.wait_ge(s_ht, NP * b + Y_ORDER.index(t // 2) + 1)
                    passes = [(part, kc) for kc in range(DC) for part in range(2)]
                    for n, (part, kc) in enumerate(passes):
                        ins = mm(bank, y_of(t // 2)[:, part, kc, t % 2 * P:(t % 2 + 1) * P], Wq1[:, kc, hf * HALF:(hf + 1) * HALF],
                                 start=n == 0, stop=n == len(passes) - 1)
                elif kind == "g":
                    t, r = a
                    if t % 2 == 0 and r == 0:
                        pe.wait_ge(s_hn, NP * b + t // 2 + 1)
                    for n in range(4):
                        col = (4 * r + n) * P
                        ins = nc.tensor.transpose(bank[:, n * P:(n + 1) * P], hid_of(t)[:, col:col + P], ident[:, :])
                elif kind == "f2":
                    t = a[0]
                    passes = [(w, r, n) for r in range(2) for n in range(4) for w in (hgh, hgl)]
                    for i, (w, r, n) in enumerate(passes):
                        if i % 8 == 0:
                            pe.wait_ge(s_hg, 2 * T * b + 2 * t + r + 1)
                        ins = mm(bank[:, 0:D], w[:, r, n * P:(n + 1) * P], Wq2[:, 4 * r + n, :],
                                 start=i == 0, stop=i == len(passes) - 1)
                elif kind == "zt":
                    i = a[0]
                    if i % (NP // 2) == 0:
                        pe.wait_ge(s_z, DC * NH * b - (i < NP // 2))
                    for j in range(2):
                        for c in range(DC):
                            toks = slice((2 * i + j) * P, (2 * i + j + 1) * P)
                            ins = nc.tensor.transpose(bank[:, j * D + c * P:j * D + (c + 1) * P], uz[:, c, toks], ident[:, :])
                elif kind == "a":
                    pe.wait_ge(s_zs, NP * (b - 1) + a[0] + 1)
                    passes = [(w, part, c) for c in range(DC) for w, part in ((W2h, 0), (W2h, 1), (W2l, 0))]
                    for j in range(2):
                        for n, (w, part, c) in enumerate(passes):
                            ins = mm(bank[:, j * D:(j + 1) * D], z_of(a[0])[:, part, c, j * P:(j + 1) * P], w[:, c, :],
                                     start=n == 0, stop=n == len(passes) - 1)
                ins.then_inc(s_fill[k], 1)

            def setup_step(g):
                if g == 3:
                    pe.wait_ge(s_bc, 1)
                    wait_evacuated(pe, -1, last_filler(0))
                    for c in range(DC):
                        mm(FP[:, 0, 0:D], onesm[:, :], w2g[:, c * D:(c + 1) * D], start=c == 0, stop=c == DC - 1)
                    for c in range(DC):
                        ins = mm(FP[:, 0, D:2 * D], bcasts[:, c, :], w2raw[:, c * D:(c + 1) * D], start=c == 0, stop=c == DC - 1)
                    ins.then_inc(s_cmm, 1)
                elif g == 5:
                    pe.wait_ge(s_tern, 1)
                    wait_evacuated(pe, -1, last_filler(1))
                    for c in range(HC):
                        ins = mm(FP[:, 1, 0:D], bcasts[:, DC + c, :], Wq2[:, c, :].bitcast(F32), start=c == 0, stop=c == HC - 1)
                    ins.then_inc(s_cmm, 1)
                    pe.wait_ge(s_tern, 2)
                    for h in range(2):
                        pe.wait_ge(s_setup, 1 + h)
                        for c in range(DC):
                            ins = mm(FP[:, h, :], bcasts[:, DC + HC + c, :], Wq1[:, c, h * HALF:(h + 1) * HALF].bitcast(F32),
                                     start=c == 0, stop=c == DC - 1)
                        ins.then_inc(s_cmm, 1)

            def body(b, first=False, last=False):
                for g in range(GROUPS):
                    scores(b, g, first)
                    if g == 0 and not first:
                        times_v(b - 1, GROUPS - 1, False)
                    if first:
                        setup_step(g)
                    for s in steps(g, first, last):
                        step(b, *s)
                    if g:
                        times_v(b, g - 1, first)

            pe.wait_ge(s_ident, 1)
            for s in PRO:
                if s == [s for s in PRO if s[0] in ("k", "q", "v")][0]:
                    pe.wait_ge(s_w1s, 1)
                step(-1, *s)
            pe.wait_ge(s_abs, 2)
            pe.wait_ge(s_ones, 1)
            mm(OP[:, 1, 0:2], ones[:, :], asum[:, :], start=True, stop=True).then_inc(s_tot, 1)
            body(0, first=True)
            with pe.Fori(1, NB - 1) as b:
                body(b)
            body(NB - 1, last=True)
            times_v(NB - 1, GROUPS - 1, False, last=True)
            for s in EPI:
                step(NB, *s)



def kernel(L0_attn_x, L0_attn_W1, L0_attn_b1, L0_attn_W2, L0_attn_b2, L0_attn_gamma, L0_attn_beta,
           L0_ffn_ln1_g, L0_ffn_ln1_b, L0_ffn_w1, L0_ffn_b1, L0_ffn_ln2_g, L0_ffn_ln2_b, L0_ffn_w2, L0_ffn_b2):
    import numpy as _np
    import concourse.bacc as _bacc
    from concourse import mybir as _mybir
    from concourse.bass_utils import run_bass_kernel_spmd as _run

    def columns(v):
        return _np.ascontiguousarray(_np.asarray(v).reshape(-1, P).T)

    arrays = {
        "x": _np.ascontiguousarray(L0_attn_x),
        "W1": _np.ascontiguousarray(L0_attn_W1),
        "b1": _np.ascontiguousarray(L0_attn_b1),
        "b1c": columns(L0_attn_b1),
        "W2": _np.ascontiguousarray(L0_attn_W2),
        "b2": _np.ascontiguousarray(L0_attn_b2),
        "gamc": columns(L0_attn_gamma),
        "betc": columns(L0_attn_beta),
        "l1gc": columns(L0_ffn_ln1_g),
        "l1bc": columns(L0_ffn_ln1_b),
        "w1T": _np.ascontiguousarray(_np.asarray(L0_ffn_w1).T),
        "fb1": _np.ascontiguousarray(L0_ffn_b1),
        "l2gc": columns(L0_ffn_ln2_g),
        "l2bc": columns(L0_ffn_ln2_b),
        "w2T": _np.ascontiguousarray(_np.asarray(L0_ffn_w2).T),
        "fb2": _np.ascontiguousarray(L0_ffn_b2),
    }
    nc = _bacc.Bacc("TRN2", target_bir_lowering=False, num_devices=1)
    args = [nc.dram_tensor(f"in_{n}", a.shape, _mybir.dt.from_np(a.dtype), kind="ExternalInput").ap()
            for n, a in arrays.items()]
    out = nc.dram_tensor("out_dram", (NB, SEQ, D), _mybir.dt.float32, kind="ExternalOutput").ap()
    hybrid_block_kernel(nc, *args, out)
    r = _run(nc, [{f"in_{n}": a for n, a in arrays.items()}], core_ids=[0])
    return r.results[0]["out_dram"]
```
